# Optimizing a Trainium2 kernel written in Bass

```python
import numpy as np
import jax
import jax.numpy as jnp

def _softmax(x, axis=-1):
    return jax.nn.softmax(x, axis=axis)

def _gelu(x):
    return jax.nn.gelu(x, approximate=True)

def _silu(x):
    return jax.nn.silu(x)

def _sigmoid(x):
    return jax.nn.sigmoid(x)

def _layernorm(x, axis=-1, eps=1e-05):
    m = jnp.mean(x, axis=axis, keepdims=True)
    v = jnp.var(x, axis=axis, keepdims=True)
    return (x - m) / jnp.sqrt(v + eps)

def _scatter_add(tgt, idx, src, axis=0):
    return tgt.at[idx].add(src)

def _segment_sum(src, seg, n):
    return jax.ops.segment_sum(src, seg, n)
kernel_name = 'mk_gnn_preln_d2_gnn_r32_00d7a8'

def setup_inputs(seed: int=0):
    np.random.seed(seed)
    _w = jnp.asarray

    def _rec_inputs():
        import jax
        import jax.numpy as jnp
        _gk = jax.random.key(seed)
        x = -0.000202 + 1 * jax.random.normal(jax.random.fold_in(_gk, 1), (3125, 64), jnp.float32)
        _s = jax.random.randint(jax.random.fold_in(_gk, 2), (25000,), 0, 3125, jnp.int32)
        _d = jax.random.randint(jax.random.fold_in(_gk, 3), (25000,), 0, 3125, jnp.int32)
        _loop = jnp.arange(3125, dtype=jnp.int32)
        src = jnp.concatenate([_s, _d, _loop])
        dst = jnp.concatenate([_d, _s, _loop])
        _o = jnp.argsort(dst, stable=True)
        src = src[_o]
        dst = dst[_o]
        edge_attr_64 = -9.77346e-05 + 0.999888 * jax.random.normal(jax.random.fold_in(_gk, 12), (53125, 64), jnp.float32)
        return (x, src, dst, edge_attr_64)
    x, src, dst, edge_attr_64 = _rec_inputs()

    def _L0_gnn_setup():
        import jax, jax.numpy as jnp
        import numpy as np
        N = 3125
        E = 50000
        HIDDEN = 64
        OUT = 64
        MID = 2 * OUT

        def gcn_conv(x, edge_index, W, b, num_nodes):
            row, col = (edge_index[0], edge_index[1])
            loop = jnp.arange(num_nodes, dtype=row.dtype)
            row = jnp.concatenate([row, loop])
            col = jnp.concatenate([col, loop])
            deg = jax.ops.segment_sum(jnp.ones_like(col, dtype=x.dtype), col, num_segments=num_nodes)
            dis = jnp.where(deg > 0, jax.lax.rsqrt(deg), 0.0)
            norm = dis[row] * dis[col]
            xw = x @ W
            msg = xw[row] * norm[:, None]
            out = jax.ops.segment_sum(msg, col, num_segments=num_nodes)
            return out + b
        key = jax.random.key(seed)
        k1, k2, k3, k4 = jax.random.split(key, 4)
        x = jax.random.normal(k1, (N, HIDDEN), dtype=jnp.float32)
        edge_index = jax.random.randint(k2, (2, E), 0, N, dtype=jnp.int64)
        s1 = 1.0 / np.sqrt(HIDDEN)
        s2 = 1.0 / np.sqrt(MID)
        W1 = jax.random.uniform(k3, (HIDDEN, MID), dtype=jnp.float32, minval=-s1, maxval=s1)
        b1 = jnp.zeros((MID,), dtype=jnp.float32)
        W2 = jax.random.uniform(k4, (MID, OUT), dtype=jnp.float32, minval=-s2, maxval=s2)
        b2 = jnp.zeros((OUT,), dtype=jnp.float32)
        return {'x': x, 'edge_index': edge_index, 'W1': W1, 'b1': b1, 'W2': W2, 'b2': b2}
    _L0_gnn_all = _L0_gnn_setup()
    _L0_gnn_in = {k: v for k, v in _L0_gnn_all.items() if k in ('W1', 'b1', 'W2', 'b2')}
    del _L0_gnn_all

    def _L1_gnn_setup():
        import jax, jax.numpy as jnp
        import numpy as np
        N_NODES = 50000
        N_EDGES = 25000
        HID = 64

        def _mpnn_layer(h, efeat, src, dst, W_msg, b_msg, W_app, b_app, residual=True):
            h_src = h[src]
            m = jax.nn.relu(jnp.concatenate([h_src, efeat], axis=-1) @ W_msg + b_msg)
            agg = jax.ops.segment_sum(m, dst, num_segments=h.shape[0])
            h_new = jax.nn.relu(jnp.concatenate([h, agg], axis=-1) @ W_app + b_app)
            if residual:
                h_new = h_new + h
            return h_new
        key = jax.random.key(seed)
        ks = jax.random.split(key, 14)
        s = 1.0 / np.sqrt(2 * HID)
        inp = {'feat': jax.random.normal(ks[0], (N_NODES, HID), jnp.float32), 'efeat': jax.random.normal(ks[1], (N_EDGES, HID), jnp.float32), 'src': jax.random.randint(ks[2], (N_EDGES,), 0, N_NODES, jnp.int32), 'dst': jax.random.randint(ks[3], (N_EDGES,), 0, N_NODES, jnp.int32), 'W1_msg': jax.random.uniform(ks[4], (2 * HID, HID), jnp.float32, -s, s), 'b1_msg': jnp.zeros((HID,), jnp.float32), 'W1_app': jax.random.uniform(ks[5], (2 * HID, HID), jnp.float32, -s, s), 'b1_app': jnp.zeros((HID,), jnp.float32), 'W2_msg': jax.random.uniform(ks[6], (2 * HID, HID), jnp.float32, -s, s), 'b2_msg': jnp.zeros((HID,), jnp.float32), 'W2_app': jax.random.uniform(ks[7], (2 * HID, HID), jnp.float32, -s, s), 'b2_app': jnp.zeros((HID,), jnp.float32)}
        return inp
    _L1_gnn_all = _L1_gnn_setup()
    _L1_gnn_in = {k: v for k, v in _L1_gnn_all.items() if k in ('W1_msg', 'b1_msg', 'W1_app', 'b1_app', 'W2_msg', 'b2_msg', 'W2_app', 'b2_app')}
    del _L1_gnn_all
    return {'x': x, 'src': src, 'dst': dst, 'edge_attr_64': edge_attr_64, 'L0_gnn_W1': _L0_gnn_in['W1'], 'L0_gnn_b1': _L0_gnn_in['b1'], 'L0_gnn_W2': _L0_gnn_in['W2'], 'L0_gnn_b2': _L0_gnn_in['b2'], 'L1_gnn_W1_msg': _L1_gnn_in['W1_msg'], 'L1_gnn_b1_msg': _L1_gnn_in['b1_msg'], 'L1_gnn_W1_app': _L1_gnn_in['W1_app'], 'L1_gnn_b1_app': _L1_gnn_in['b1_app'], 'L1_gnn_W2_msg': _L1_gnn_in['W2_msg'], 'L1_gnn_b2_msg': _L1_gnn_in['b2_msg'], 'L1_gnn_W2_app': _L1_gnn_in['W2_app'], 'L1_gnn_b2_app': _L1_gnn_in['b2_app']}

def reference(x, src, dst, edge_attr_64, L0_gnn_W1, L0_gnn_b1, L0_gnn_W2, L0_gnn_b2, L1_gnn_W1_msg, L1_gnn_b1_msg, L1_gnn_W1_app, L1_gnn_b1_app, L1_gnn_W2_msg, L1_gnn_b2_msg, L1_gnn_W2_app, L1_gnn_b2_app):
    import jax
    import jax.numpy as jnp

    def _L0_gnn_ref(x, edge_index, W1, b1, W2, b2):
        import jax, jax.numpy as jnp
        import numpy as np
        N = 3125
        E = 50000
        HIDDEN = 64
        OUT = 64
        MID = 2 * OUT

        def gcn_conv(x, edge_index, W, b, num_nodes):
            row, col = (edge_index[0], edge_index[1])
            loop = jnp.arange(num_nodes, dtype=row.dtype)
            row = jnp.concatenate([row, loop])
            col = jnp.concatenate([col, loop])
            deg = jax.ops.segment_sum(jnp.ones_like(col, dtype=x.dtype), col, num_segments=num_nodes)
            dis = jnp.where(deg > 0, jax.lax.rsqrt(deg), 0.0)
            norm = dis[row] * dis[col]
            xw = x @ W
            msg = xw[row] * norm[:, None]
            out = jax.ops.segment_sum(msg, col, num_segments=num_nodes)
            return out + b
        h = gcn_conv(x, edge_index, W1, b1, N)
        h = jax.nn.relu(h)
        return gcn_conv(h, edge_index, W2, b2, N)

    def _L1_gnn_ref(feat, efeat, src, dst, W1_msg, b1_msg, W1_app, b1_app, W2_msg, b2_msg, W2_app, b2_app):
        import jax, jax.numpy as jnp
        import numpy as np
        N_NODES = 50000
        N_EDGES = 25000
        HID = 64

        def _mpnn_layer(h, efeat, src, dst, W_msg, b_msg, W_app, b_app, residual=True):
            h_src = h[src]
            m = jax.nn.relu(jnp.concatenate([h_src, efeat], axis=-1) @ W_msg + b_msg)
            agg = jax.ops.segment_sum(m, dst, num_segments=h.shape[0])
            h_new = jax.nn.relu(jnp.concatenate([h, agg], axis=-1) @ W_app + b_app)
            if residual:
                h_new = h_new + h
            return h_new
        h1 = _mpnn_layer(feat, efeat, src, dst, W1_msg, b1_msg, W1_app, b1_app)
        h2 = _mpnn_layer(h1, efeat, src, dst, W2_msg, b2_msg, W2_app, b2_app)
        return h2
    edge_index = jnp.stack([src, dst])
    h = jnp.maximum(_layernorm(x, axis=-1), 0.0)
    x = x + _L0_gnn_ref(h, edge_index, L0_gnn_W1, L0_gnn_b1, L0_gnn_W2, L0_gnn_b2)
    h = jnp.maximum(_layernorm(x, axis=-1), 0.0)
    x = x + _L1_gnn_ref(h, edge_attr_64, src, dst, L1_gnn_W1_msg, L1_gnn_b1_msg, L1_gnn_W1_app, L1_gnn_b1_app, L1_gnn_W2_msg, L1_gnn_b2_msg, L1_gnn_W2_app, L1_gnn_b2_app)
    return x

_drawn_inputs = setup_inputs


def setup_inputs(seed=0):
    import zlib

    import numpy as np

    out = dict(_drawn_inputs(seed))
    spreads = {'L0_gnn_b1': (0.0, 0.442),
     'L0_gnn_b2': (0.0, 0.1),
     'L1_gnn_b1_msg': (0.0, 0.1),
     'L1_gnn_b1_app': (0.0, 0.304),
     'L1_gnn_b2_msg': (0.0, 0.1),
     'L1_gnn_b2_app': (0.0, 0.385)}
    factors = {}
    for name, (base, spread) in spreads.items():
        noise = np.random.default_rng([zlib.crc32(name.encode()), seed]).standard_normal(out[name].shape)
        drawn = base * np.exp(spread * noise) if base else spread * noise
        out[name] = jnp.asarray(drawn.astype(out[name].dtype))
    for name, factor in factors.items():
        out[name] = (out[name] * factor).astype(out[name].dtype)
    return out
```

```python
import concourse.bass as bass
from concourse import mybir
from contextlib import ExitStack

P = 128
N = 3125
E = 53125
D = 64
MID = 128
NB = -(-N // P)
NTAIL = N - (NB - 1) * P
AGGB = NB + 1
TPG = 8
GE = P * TPG
NG = -(-E // GE)
ETAIL = E - (NG - 1) * GE
TFULL = ETAIL // TPG
TREST = ETAIL - TFULL * TPG
R = 4
NIT = NG // R
WIN = 2 * P
SHIFTS = -(-NB // 2) - 1
NO_NODE = 1 << 20
CB = 4
NC = -(-NB // CB)
EPS = 1e-5

fp32 = mybir.dt.float32
bf16 = mybir.dt.bfloat16
i32 = mybir.dt.int32
ALU = mybir.AluOpType
ACT = mybir.ActivationFunctionType
AX = mybir.AxisListType


def chunk(c):
    return c * CB, min(CB, NB - c * CB)


class Chain:

    def __init__(self, engine, sem):
        self.engine, self.sem, self.n = engine, sem, 0

    def __call__(self, ins):
        self.n += 1
        ins.then_inc(self.sem, 1)
        self.engine.wait_ge(self.sem, self.n)


def gnn_kernel(nc, x, src, dst, efeat, W1, b1, W2, b2,
               W1_msg, b1_msg, W1_app, b1_app, W2_msg, b2_msg, W2_app, b2_app, out):
    ctx = ExitStack()
    with ctx:
        def sb(name, shape, dt=fp32):
            return ctx.enter_context(nc.sbuf_tensor(name, shape, dt))

        def sem(name):
            return ctx.enter_context(nc.semaphore(name))

        tables = [nc.dram_tensor(f"table{i}", (P * NB, D), fp32).ap() for i in range(4)]

        src_i = sb("src_i", [P, NG, TPG], i32)
        dst_i = sb("dst_i", [P, NG, TPG], i32)
        tmp_i = sb("tmp_i", [P, NG, TPG], i32)
        row_i = sb("row_i", [P, NG + R, TPG], i32)
        dst_lo = sb("dst_lo", [P, NG, TPG])
        dst_hi = sb("dst_hi", [P, NG, TPG])
        dst_f = sb("dst_f", [P, NG, TPG])
        rel0 = sb("rel0", [P, NG, TPG])
        rel = sb("rel", [P, NG, TPG])
        outside = sb("outside", [P, NG, TPG])
        gmin = sb("gmin", [P, NG])
        bmin = sb("bmin", [NG, 1])
        bdiag = sb("bdiag", [NG, NG])
        base = sb("base", [P, NG])
        col0 = sb("col0", [1, NG], i32)
        col = sb("col", [1, NG], i32)
        far = sb("far", [P, 1])
        farT = sb("farT", [1, 1])
        flag = sb("flag", [1, 1], i32)
        idx = sb("idx", [P, R, TPG], i32)
        rows = sb("rows", [P, R, TPG * D])
        ef = sb("ef", [P, R, TPG * D])
        efT = sb("efT", [P, 2, 4 * P])
        msg = sb("msg", [P, 2, TPG * D])
        onehot = sb("onehot", [P, 2, TPG, WIN])
        iota_i = sb("iota_i", [P, WIN], i32)
        iota_f = sb("iota_f", [P, WIN])
        iota_b = sb("iota_b", [P, P], bf16)
        part_i = sb("part_i", [P, 1], i32)
        part_f = sb("part_f", [P, 1])
        ident = sb("ident", [P, P])
        zeros_b = sb("zeros_b", [P, 512], bf16)
        ones = sb("ones", [P, P])
        hot_lo = sb("hot_lo", [P, 2, TPG, P], bf16)
        hot_hi = sb("hot_hi", [P, 2, TPG, AGGB], bf16)
        dis = sb("dis", [P, NB])
        xs = sb("xs", [P, NB, D])
        cat = sb("cat", [P, NB, 2 * D])
        tab = sb("tab", [P, NB, D])
        work = sb("work", [P, NB, D])
        stat = sb("stat", [P, 4, NB])
        eps = sb("eps", [P, 1])
        catT = sb("catT", [P, NB * P])
        midT = sb("midT", [P, NB * P])
        W1_s = sb("W1_s", [D, MID])
        W2_s = sb("W2_s", [MID, D])
        b1_s = sb("b1_s", [MID, 1])
        b2_s = sb("b2_s", [P, D])
        top_s = sb("top_s", [D, 2, D])
        bot_s = sb("bot_s", [P, 2, P])
        app_s = sb("app_s", [P, 2, D])
        bmsg_s = sb("bmsg_s", [P, 2, D])
        bapp_s = sb("bapp_s", [P, 2, D])

        agg = ctx.enter_context(nc.psum_tensor("agg", [P, 2048], fp32))
        tp = ctx.enter_context(nc.psum_tensor("tp", [P, 2, 512], fp32))
        mm = ctx.enter_context(nc.psum_tensor("mm", [P, 2, 512], fp32))
        iota = tp[:, 1, 0:WIN]

        def agg_chunk(c):
            k, n = chunk(c)
            return agg[:, k * D:(k + n) * D].rearrange("p (k d) -> p k d", d=D)

        staged = sem("staged")
        started = sem("started")
        gathered = [sem(f"gathered{j}") for j in range(R)]
        loaded = [sem(f"loaded{j}") for j in range(R)]
        hot_ready = sem("hot_ready")
        summed = sem("summed")
        turned = sem("turned")
        copied = sem("copied")
        projected = sem("projected")
        added = sem("added")
        msg_ready = sem("msg_ready")
        edge_sems = [staged, started, *loaded, hot_ready, summed, turned, copied, projected, added, msg_ready]

        def edge_pass(table, layer):
            with nc.Block() as block:
                @block.gpsimd
                def _(pool):
                    with pool.Fori(0, NIT) as it:
                        for j in range(R):
                            pool.wait_ge(staged, it * R + (j + 1))
                            pool.sem_inc(started, 1)
                            for t in range(TPG):
                                nc.gpsimd.indirect_dma_start(
                                    out=rows[:, j, t * D:(t + 1) * D], out_offset=None, in_=table[:, :],
                                    in_offset=bass.IndirectOffsetOnAxis(ap=idx[:, j, t:t + 1], axis=0),
                                ).then_inc(gathered[j], 16)
                    for j in range(R):
                        pool.wait_ge(gathered[j], NIT * TPG * 16)

                @block.sync
                def _(sp):
                    if layer is None:
                        return

                    def load(g, j):
                        sp.dma_start(ef[:, j, :], efeat[bass.ds(g * GE, GE), :].rearrange(
                            "(p t) f -> p (t f)", t=TPG)).then_inc(loaded[j], 16)

                    for j in range(R):
                        load(j, j)
                    with sp.Fori(1, NIT - 1) as it:
                        for j in range(R):
                            sp.wait_ge(turned, (it - 1) * R + (j + 1))
                            load(it * R + j, j)
                    for j in range(R):
                        sp.wait_ge(turned, (NIT - 2) * R + j + 1)
                        if j < R - 1:
                            load((NIT - 1) * R + j, j)
                    e0 = (NG - 1) * GE
                    sp.dma_start(ef[0:TFULL, R - 1, :], efeat[e0:e0 + TFULL * TPG, :].rearrange(
                        "(p t) f -> p (t f)", t=TPG)).then_inc(loaded[R - 1], 16)
                    sp.dma_start(ef[TFULL:TFULL + 1, R - 1, 0:TREST * D], efeat[E - TREST:E, :].rearrange(
                        "(p t) f -> p (t f)", t=TREST)).then_inc(loaded[R - 1], 16)

                @block.vector
                def _(dve):
                    def stage(g, j):
                        nc.vector.tensor_copy(idx[:, j:j + 1, :], row_i[:, bass.ds(g, 1), :]).then_inc(staged, 1)

                    def one_hot(g, j):
                        for t in range(TPG):
                            last = nc.vector.tensor_scalar(
                                onehot[:, j % 2, t, :], iota, rel[:, bass.ds(g, 1), t:t + 1].rearrange("p a b -> p (a b)"),
                                None, ALU.is_equal)
                        last.then_inc(hot_ready, 1)

                    def step(g, j, first):
                        if first and j < 2:
                            one_hot(g, j)
                        else:
                            dve.wait_ge(summed, g - 1)
                            one_hot(g, j)
                        if layer is None:
                            if not (first and j == 0):
                                dve.wait_ge(summed, g)
                                stage(g + (R - 1), (j - 1) % R)
                        else:
                            dve.wait_ge(projected, g + 1)
                            dve.wait_ge(gathered[j], (g - j) * (TPG * 16 // R) + TPG * 16)
                            nc.vector.tensor_tensor(msg[:, j % 2, :], mm[:, j % 2, :], rows[:, j, :],
                                                    ALU.add).then_inc(added, 1)
                            dve.wait_ge(added, g + 1)
                            stage(g + R, j)

                    for j in range(R):
                        stage(j, j)
                    for j in range(R):
                        step(j, j, True)
                    with dve.Fori(1, NIT) as it:
                        for j in range(R):
                            step(it * R + j, j, False)

                @block.scalar
                def _(act):
                    if layer is None:
                        return

                    def copy(g, b):
                        act.wait_ge(turned, g + 1)
                        nc.scalar.copy(efT[:, b, :], tp[:, 0, :]).then_inc(copied, 1)

                    def relu(g, b):
                        act.wait_ge(added, g + 1)
                        nc.scalar.activation(msg[:, b, :], msg[:, b, :], ACT.Relu).then_inc(msg_ready, 1)

                    copy(0, 0)
                    with act.Fori(0, NIT - 1) as it:
                        for j in range(R):
                            copy(it * R + (j + 1), (j + 1) % 2)
                            relu(it * R + j, j % 2)
                    for j in range(R):
                        g = (NIT - 1) * R + j
                        if g + 1 < NG:
                            copy(g + 1, (j + 1) % 2)
                        relu(g, j % 2)

                @block.tensor
                def _(pe):
                    def turn(g, j, count):
                        pe.wait_ge(loaded[j], count)
                        for q in range(TPG // 2):
                            last = nc.tensor.transpose(tp[:, 0, q * P:(q + 1) * P],
                                                       ef[:, j, q * P:(q + 1) * P], ident[:])
                        last.then_inc(turned, 1)

                    def project(g, j):
                        pe.wait_ge(copied, g + 1)
                        for q in range(TPG // 2):
                            last = nc.tensor.matmul(mm[:, j % 2, q * P:(q + 1) * P],
                                                    lhsT=efT[:, j % 2, q * P:(q + 1) * P], rhs=bot_s[:, layer, :],
                                                    start=True, stop=True)
                        last.then_inc(projected, 1)

                    def scatter(g, j, at):
                        pe.wait_ge(hot_ready, g + 1)
                        if layer is None:
                            pe.wait_ge(gathered[j], (g - j) * (TPG * 16 // R) + TPG * 16)
                            values = rows[:, j, :]
                        else:
                            pe.wait_ge(msg_ready, g + 1)
                            values = msg[:, j % 2, :]
                        for w in range(2):
                            for t in range(TPG):
                                last = nc.tensor.matmul(agg[:, bass.ds(at + w * D, D)],
                                                        lhsT=onehot[:, j % 2, t, w * P:(w + 1) * P],
                                                        rhs=values[:, t * D:(t + 1) * D],
                                                        start=False, stop=True, skip_group_check=True)
                        last.then_inc(summed, 1)

                    def columns(g0):
                        return [pe.value_load(col[0:1, bass.ds(g0 + j, 1)], min_val=0, max_val=(NB - 1) * D)
                                for j in range(R)]

                    if layer is None:
                        with pe.Fori(0, NIT) as it:
                            at = columns(it * R)
                            for j in range(R):
                                scatter(it * R + j, j, at[j])
                        return
                    turn(0, 0, 16)
                    project(0, 0)
                    with pe.Fori(0, NIT - 1) as it:
                        at = columns(it * R)
                        for j in range(R):
                            n = (j + 1) % R
                            turn(it * R + (j + 1), n, it * 16 + (16 if j < R - 1 else 32))
                            scatter(it * R + j, j, at[j])
                            project(it * R + (j + 1), n)
                    at = columns((NIT - 1) * R)
                    for j in range(R):
                        g = (NIT - 1) * R + j
                        if g + 1 < NG:
                            turn(g + 1, j + 1, NIT * 16 + (16 if g + 1 == NG - 1 else 0))
                        scatter(g, j, at[j])
                        if g + 1 < NG:
                            project(g + 1, j + 1)

        def zero_sums():
            for b in range(0, AGGB * D, 512):
                n = min(512, AGGB * D - b)
                last = nc.tensor.matmul(agg[:, b:b + n], lhsT=zeros_b[:, 0:P], rhs=zeros_b[:, 0:n],
                                        start=True, stop=True, skip_group_check=True)
            return last

        def clear_edge_sems(sp):
            for s in edge_sems:
                sp.sem_clear(s)

        def clear_gather_sems(pool):
            pool.dma_reset(range(gathered[0].num, gathered[-1].num + 1))
            for s in gathered:
                pool.sem_clear(s)

        s_shift = sem("s_shift")

        def sum_over_edges(table, layer):
            edge_pass(table, layer)
            outlying = nc.values_load(flag[0:1, 0:1], min_val=0, max_val=1)
            with nc.If(outlying > 0):
                with nc.Fori(0, SHIFTS):
                    with nc.Block() as block:
                        @block.sync
                        def _(sp):
                            clear_edge_sems(sp)

                        @block.gpsimd
                        def _(pool):
                            clear_gather_sems(pool)

                        @block.vector
                        def _(dve):
                            nc.vector.tensor_scalar(rel[:], rel[:], float(-WIN), None, ALU.add)
                            nc.vector.tensor_scalar(col[:], col[:], 2 * D, (NB - 1) * D, ALU.add, ALU.min)
                    edge_pass(table, layer)

        def bcast(ap, n):
            return ap.unsqueeze(2).to_broadcast([P, ap.shape[1], n])

        def layer_norm(dve, chain, s_sqrt_in, s_sqrt_out):
            mean, var, std, rstd = (stat[:, i, :] for i in range(4))
            chain(nc.vector.tensor_reduce(mean, xs[:], AX.X, ALU.add))
            chain(nc.vector.tensor_scalar(mean, mean, 1.0 / D, None, ALU.mult))
            chain(nc.vector.tensor_tensor(work[:], xs[:], bcast(mean, D), ALU.subtract))
            chain(nc.vector.tensor_tensor(tab[:], work[:], work[:], ALU.mult))
            chain(nc.vector.tensor_reduce(var, tab[:], AX.X, ALU.add))
            chain(nc.vector.tensor_scalar(var, var, 1.0 / D, EPS, ALU.mult, ALU.add))
            nc.vector.tensor_copy(std, var).then_inc(s_sqrt_in, 1)
            dve.wait_ge(s_sqrt_out, 1)
            chain(nc.vector.reciprocal(rstd, std))
            chain(nc.vector.tensor_tensor(work[:], work[:], bcast(rstd, D), ALU.mult))

        s_idx = sem("s_idx"); s_x = sem("s_x"); s_w = sem("s_w"); s_fill = sem("s_fill"); s_io = sem("s_io")
        s_dve = sem("s_dve"); s_sq = sem("s_sq"); s_sqd = sem("s_sqd")
        s_hot = sem("s_hot"); s_deg = sem("s_deg"); s_const = sem("s_const");
        s_gm = sem("s_gm"); s_gt = sem("s_gt"); s_bd = sem("s_bd"); s_bb = sem("s_bb")
        s_far = sem("s_far"); s_ft = sem("s_ft");
        s_tab = sem("s_tab"); s_out = sem("s_out")

        def bias_rows(b):
            return b.rearrange("(a n) -> a n", a=1).to_broadcast([P, D])

        with nc.Block() as block:
            @block.sync
            def _(sp):
                sp.wait_ge(s_fill, 1)
                for to, of in ((dst_i, dst), (src_i, src)):
                    full = (NG - 1) * GE
                    sp.dma_start(to[:, 0:NG - 1, :], of[0:full].rearrange("(g p t) -> p g t", p=P, t=TPG)
                                 ).then_inc(s_idx, 16)
                    sp.dma_start(to[0:TFULL, NG - 1:NG, :], of[full:full + TFULL * TPG].rearrange(
                        "(p g t) -> p g t", g=1, t=TPG)).then_inc(s_idx, 16)
                    sp.dma_start(to[TFULL:TFULL + 1, NG - 1:NG, 0:TREST], of[E - TREST:E].rearrange(
                        "(p g t) -> p g t", p=1, g=1)).then_inc(s_idx, 16)
                sp.wait_ge(s_tab, 1)
                sp.dma_start(tables[0].rearrange("(p k) d -> p k d", k=NB), tab[:, :, :]).then_inc(s_out, 16)
                sp.wait_ge(s_out, 16)

            @block.scalar
            def _(act):
                act.wait_ge(s_fill, 1)
                act.dma_start(xs[:, 0:NB - 1, :], x[0:(NB - 1) * P, :].rearrange("(k p) d -> p k d", p=P)
                              ).then_inc(s_x, 16)
                act.dma_start(xs[0:NTAIL, NB - 1, :], x[(NB - 1) * P:N, :]).then_inc(s_x, 16)
                act.dma_start(W1_s[:], W1).then_inc(s_w, 16)
                act.dma_start(W2_s[:], W2).then_inc(s_w, 16)
                act.dma_start(b1_s[:], b1.rearrange("(p a) -> p a", a=1)).then_inc(s_w, 16)
                act.dma_start(b2_s[:], bias_rows(b2)).then_inc(s_w, 16)
                for l, (wm, bm, wa, ba) in enumerate(((W1_msg, b1_msg, W1_app, b1_app),
                                                      (W2_msg, b2_msg, W2_app, b2_app))):
                    act.dma_start(top_s[:, l, :], wm[0:D, :]).then_inc(s_w, 16)
                    act.dma_start(bot_s[0:D, l, 0:D], wm[D:2 * D, :]).then_inc(s_w, 16)
                    act.dma_start(bot_s[D:P, l, D:P], wm[D:2 * D, :]).then_inc(s_w, 16)
                    act.dma_start(app_s[:, l, :], wa).then_inc(s_w, 16)
                    act.dma_start(bmsg_s[:, l, :], bias_rows(bm)).then_inc(s_w, 16)
                    act.dma_start(bapp_s[:, l, :], bias_rows(ba)).then_inc(s_w, 16)
                act.wait_ge(s_sq, 1)
                nc.scalar.activation(stat[:, 2, :], stat[:, 2, :], ACT.Sqrt).then_inc(s_sqd, 1)
                act.wait_ge(s_sq, 2)
                nc.scalar.activation(dis[:], dis[:], ACT.Sqrt).then_inc(s_sqd, 1)
                act.wait_ge(s_w, 16 * 16)

            @block.gpsimd
            def _(pool):
                nc.gpsimd.iota(iota_i[:], [[1, WIN]], base=0, channel_multiplier=0).then_inc(s_io, 1)
                nc.gpsimd.iota(part_i[:], [[1, 1]], base=0, channel_multiplier=1).then_inc(s_io, 1)

            @block.vector
            def _(dve):
                chain = Chain(dve, s_dve)
                nc.vector.memset(src_i[:, NG - 1, :], 0)
                nc.vector.memset(dst_i[:, NG - 1, :], NO_NODE)
                nc.vector.memset(xs[:, NB - 1, :], 0.0)
                nc.vector.memset(bot_s[:], 0.0).then_inc(s_fill, 1)
                nc.vector.memset(cat[:], 0.0)
                nc.vector.memset(row_i[:], 0)
                nc.vector.memset(ef[:, R - 1, :], 0.0)
                nc.vector.memset(zeros_b[:], 0.0)
                nc.vector.memset(ones[:], 1.0)
                dve.wait_ge(s_io, 2)
                nc.vector.tensor_copy(iota_f[:], iota_i[:])
                nc.vector.tensor_copy(iota_b[:], iota_i[:, 0:P])
                chain(nc.vector.tensor_copy(part_f[:], part_i[:]))
                nc.vector.tensor_scalar(ident[:], iota_f[:, 0:P], part_f[:], None, ALU.is_equal).then_inc(s_const, 1)
                dve.wait_ge(s_idx, 96)
                nc.vector.tensor_copy(dst_f[:], dst_i[:])
                chain(nc.vector.tensor_scalar(tmp_i[:], dst_i[:], 7, None, ALU.arith_shift_right))
                chain(nc.vector.tensor_copy(dst_hi[:], tmp_i[:]))
                chain(nc.vector.tensor_scalar(tmp_i[:], dst_i[:], P - 1, None, ALU.bitwise_and))
                chain(nc.vector.tensor_copy(dst_lo[:], tmp_i[:]))
                iota_hi = iota_f[:, 0:AGGB].unsqueeze(1).to_broadcast([P, TPG, AGGB])
                for g in range(2):
                    nc.vector.tensor_tensor(hot_hi[:, g, :, :], iota_hi, dst_hi[:, g, :].unsqueeze(2).to_broadcast(
                        [P, TPG, AGGB]), ALU.is_equal)
                    for t in range(TPG):
                        last = nc.vector.tensor_scalar(hot_lo[:, g, t, :], iota_b[:], dst_lo[:, g, t:t + 1], None,
                                                       ALU.is_equal)
                    last.then_inc(s_hot, 1)
                with dve.Fori(1, NG // 2) as it:
                    for b in range(2):
                        g = it * 2 + b
                        dve.wait_ge(s_deg, g - 1)
                        nc.vector.tensor_tensor(
                            hot_hi[:, b, :, :], iota_hi, dst_hi[:, bass.ds(g, 1), :].rearrange("p a t -> p (a t)")
                            .unsqueeze(2).to_broadcast([P, TPG, AGGB]), ALU.is_equal)
                        for t in range(TPG):
                            last = nc.vector.tensor_scalar(
                                hot_lo[:, b, t, :], iota_b[:],
                                dst_lo[:, bass.ds(g, 1), t:t + 1].rearrange("p a b -> p (a b)"), None, ALU.is_equal)
                        last.then_inc(s_hot, 1)
                chain(nc.vector.tensor_scalar(tmp_i[:], src_i[:], P - 1, None, ALU.bitwise_and))
                chain(nc.vector.tensor_scalar(tmp_i[:], tmp_i[:], NB, None, ALU.mult))
                chain(nc.vector.tensor_scalar(src_i[:], src_i[:], 7, None, ALU.arith_shift_right))
                chain(nc.vector.tensor_tensor(row_i[:, 0:NG, :], src_i[:], tmp_i[:], ALU.add))
                nc.vector.tensor_reduce(gmin[:], dst_hi[:], AX.X, ALU.min).then_inc(s_gm, 1)
                dve.wait_ge(s_gt, 1)
                chain(nc.vector.tensor_reduce(bmin[:], tp[0:NG, 0, 0:P], AX.X, ALU.min))
                nc.vector.tensor_scalar(bdiag[:], ident[0:NG, 0:NG], bmin[:], None, ALU.mult).then_inc(s_bd, 1)
                dve.wait_ge(s_bb, 1)
                chain(nc.vector.tensor_scalar(base[:], mm[:, 1, 0:NG], float(P), None, ALU.mult))
                nc.vector.tensor_scalar(col0[:], mm[0:1, 1, 0:NG], float(D), None, ALU.mult)
                nc.vector.tensor_scalar(col[:], mm[0:1, 1, 0:NG], float(D), None, ALU.mult)
                chain(nc.vector.tensor_tensor(rel0[:], dst_f[:], bcast(base[:], TPG), ALU.subtract))
                nc.vector.tensor_copy(rel[:], rel0[:])
                chain(nc.vector.tensor_scalar(outside[:], dst_f[:], float(NO_NODE), None, ALU.is_lt))
                chain(nc.vector.scalar_tensor_tensor(outside[:], rel0[:], float(WIN), outside[:], ALU.is_ge, ALU.mult))
                nc.vector.tensor_reduce(far[:], outside[:], AX.XY, ALU.max).then_inc(s_far, 1)
                dve.wait_ge(s_ft, 1)
                chain(nc.vector.tensor_copy(farT[:], mm[0:1, 1, 128:129]))
                nc.vector.tensor_scalar(flag[:], farT[:], 0.0, None, ALU.is_gt)
                dve.wait_ge(s_x, 32)
                layer_norm(dve, chain, s_sq, s_sqd)
                chain(nc.vector.tensor_scalar(work[:], work[:], 0.0, None, ALU.max))
                dve.wait_ge(s_deg, NG)
                nc.vector.tensor_scalar(dis[:], mm[:, 0, 0:NB], 1.0, None, ALU.add).then_inc(s_sq, 1)
                dve.wait_ge(s_sqd, 2)
                chain(nc.vector.reciprocal(dis[:], dis[:]))
                nc.vector.tensor_tensor(tab[:], work[:], bcast(dis[:], D), ALU.mult).then_inc(s_tab, 1)
                nc.vector.tensor_copy(iota, iota_f[:])

            @block.tensor
            def _(pe):
                pe.wait_ge(s_const, 1)
                nc.tensor.matmul(mm[:, 0, 0:AGGB], lhsT=zeros_b[:, 0:P], rhs=zeros_b[:, 0:AGGB], start=True, stop=True)
                with pe.Fori(0, NG // 2) as it:
                    for b in range(2):
                        pe.wait_ge(s_hot, it * 2 + (b + 1))
                        for t in range(TPG):
                            last = nc.tensor.matmul(mm[:, 0, 0:AGGB], lhsT=hot_lo[:, b, t, :], rhs=hot_hi[:, b, t, :],
                                                    start=False, stop=True, skip_group_check=True)
                        last.then_inc(s_deg, 1)
                pe.wait_ge(s_gm, 1)
                nc.tensor.transpose(tp[0:NG, 0, 0:P], gmin[:], ident[:]).then_inc(s_gt, 1)
                pe.wait_ge(s_bd, 1)
                nc.tensor.matmul(mm[:, 1, 0:NG], lhsT=ones[0:NG, :], rhs=bdiag[:], start=True, stop=True).then_inc(s_bb, 1)
                pe.wait_ge(s_far, 1)
                nc.tensor.matmul(mm[0:1, 1, 128:129], lhsT=far[:], rhs=ones[:, 0:1], start=True, stop=True).then_inc(s_ft, 1)
                zero_sums()

        def node_sems(name):
            return {k: sem(f"{name}_{k}") for k in ("dve", "ready", "turned", "copied", "mid", "relu", "done", "final", "out")}

        def turn_chunk(q, c, source, wide):
            k0, n = chunk(c)
            for i in range(n):
                last = nc.tensor.transpose(tp[0:(2 * D if wide else D), c % 2, i * P:(i + 1) * P],
                                           source[:, k0 + i, :], ident[:])
            last.then_inc(q["turned"], 1)

        def copy_chunk(q, c, wide):
            k0, n = chunk(c)
            h = 2 * D if wide else D
            nc.scalar.copy(catT[0:h, k0 * P:(k0 + n) * P], tp[0:h, c % 2, 0:n * P]).then_inc(q["copied"], 1)

        def product_chunk(q, c, weights, rows_):
            k0, n = chunk(c)
            for i in range(n):
                last = nc.tensor.matmul(mm[:, c % 2, i * D:(i + 1) * D], lhsT=catT[0:rows_, (k0 + i) * P:(k0 + i + 1) * P],
                                        rhs=weights, start=True, stop=True)
            last.then_inc(q["done"], 1)

        def product(c):
            n = chunk(c)[1]
            return mm[:, c % 2, 0:n * D].rearrange("p (k d) -> p k d", d=D)

        def over(bias, n):
            return bias.unsqueeze(1).to_broadcast([P, n, D])

        def pe_sweep(pe, q, source, weights, wide, before=None):
            for c in range(NC + 1):
                if c < NC:
                    pe.wait_ge(q["ready"], c + 1)
                    if c >= 2:
                        pe.wait_ge(q["copied"], c - 1)
                    elif before is not None:
                        pe.wait_ge(before["copied"], NC)
                    turn_chunk(q, c, source, wide)
                if c >= 1:
                    pe.wait_ge(q["copied"], c)
                    if c >= 3:
                        pe.wait_ge(q["final"], c - 2)
                    elif before is not None:
                        pe.wait_ge(before["final"], NC)
                    product_chunk(q, c - 1, weights, 2 * D if wide else D)

        def act_sweep(act, q, wide):
            for c in range(NC):
                act.wait_ge(q["turned"], c + 1)
                copy_chunk(q, c, wide)

        def store_table(sp, q, table):
            view = table.rearrange("(p k) d -> p k d", k=NB)
            for c in range(NC):
                k0, n = chunk(c)
                sp.wait_ge(q["final"], c + 1)
                sp.dma_start(view[:, k0:k0 + n, :], tab[:, k0:k0 + n, :]).then_inc(q["out"], 16)
            sp.wait_ge(q["out"], 16 * NC)

        def first_windows():
            nc.vector.tensor_copy(iota, iota_f[:])
            nc.vector.tensor_copy(rel[:], rel0[:])
            nc.vector.tensor_copy(col[:], col0[:])

        sum_over_edges(tables[0], None)
        q = node_sems("gcn1")
        with nc.Block() as block:
            @block.sync
            def _(sp):
                clear_edge_sems(sp)
                store_table(sp, q, tables[1])

            @block.gpsimd
            def _(pool):
                clear_gather_sems(pool)

            @block.vector
            def _(dve):
                chain = Chain(dve, q["dve"])
                for c in range(NC):
                    k0, n = chunk(c)
                    w = work[:, k0:k0 + n, :]
                    chain(nc.vector.tensor_tensor(w, agg_chunk(c), tab[:, k0:k0 + n, :], ALU.add))
                    nc.vector.tensor_tensor(w, w, bcast(dis[:, k0:k0 + n], D), ALU.mult).then_inc(q["ready"], 1)
                for c in range(NC):
                    k0, n = chunk(c)
                    dve.wait_ge(q["done"], c + 1)
                    nc.vector.tensor_tensor(tab[:, k0:k0 + n, :], agg[:, c % 4 * 512:c % 4 * 512 + n * D].rearrange(
                        "p (k d) -> p k d", d=D), bcast(dis[:, k0:k0 + n], D), ALU.mult).then_inc(q["final"], 1)
                first_windows()

            @block.scalar
            def _(act):
                for c in range(NC + 1):
                    if c < NC:
                        act.wait_ge(q["turned"], c + 1)
                        copy_chunk(q, c, False)
                    if c >= 1:
                        k0, n = chunk(c - 1)
                        act.wait_ge(q["mid"], c)
                        nc.scalar.activation(midT[:, k0 * P:(k0 + n) * P], mm[:, (c - 1) % 2, 0:n * P], ACT.Relu,
                                             bias=b1_s[:]).then_inc(q["relu"], 1)

            @block.tensor
            def _(pe):
                for c in range(NC + 2):
                    if c < NC:
                        pe.wait_ge(q["ready"], c + 1)
                        if c >= 2:
                            pe.wait_ge(q["copied"], c - 1)
                        turn_chunk(q, c, work, False)
                    if 1 <= c <= NC:
                        k0, n = chunk(c - 1)
                        pe.wait_ge(q["copied"], c)
                        if c >= 3:
                            pe.wait_ge(q["relu"], c - 2)
                        nc.tensor.matmul(mm[:, (c - 1) % 2, 0:n * P], lhsT=W1_s[:], rhs=catT[0:D, k0 * P:(k0 + n) * P],
                                         start=True, stop=True).then_inc(q["mid"], 1)
                    if c >= 2:
                        k0, n = chunk(c - 2)
                        pe.wait_ge(q["relu"], c - 1)
                        pe.wait_ge(q["ready"], min(NC, 2 * (c - 1)))
                        if c >= 6:
                            pe.wait_ge(q["final"], c - 5)
                        for i in range(n):
                            k = k0 + i
                            at = (c - 2) % 4 * 512 + i * D
                            last = nc.tensor.matmul(agg[:, at:at + D], lhsT=midT[:, k * P:(k + 1) * P],
                                                    rhs=W2_s[:], start=True, stop=True, skip_group_check=True)
                        last.then_inc(q["done"], 1)
                pe.wait_ge(q["final"], NC)
                zero_sums()

        sum_over_edges(tables[1], None)
        q2 = node_sems("gcn2")
        s_sq2, s_sqd2 = sem("s_sq2"), sem("s_sqd2")
        with nc.Block() as block:
            @block.sync
            def _(sp):
                clear_edge_sems(sp)
                store_table(sp, q2, tables[2])

            @block.gpsimd
            def _(pool):
                clear_gather_sems(pool)

            @block.vector
            def _(dve):
                chain = Chain(dve, q2["dve"])
                sums = agg[:, 0:NB * D].rearrange("p (k d) -> p k d", d=D)
                chain(nc.vector.tensor_tensor(work[:], sums, tab[:], ALU.add))
                chain(nc.vector.tensor_tensor(work[:], work[:], bcast(dis[:], D), ALU.mult))
                chain(nc.vector.tensor_tensor(work[:], work[:], over(b2_s[:], NB), ALU.add))
                chain(nc.vector.tensor_tensor(xs[:], xs[:], work[:], ALU.add))
                layer_norm(dve, chain, s_sq2, s_sqd2)
                for c in range(NC):
                    k0, n = chunk(c)
                    nc.vector.tensor_scalar(cat[:, k0:k0 + n, 0:D], work[:, k0:k0 + n, :], 0.0, None,
                                            ALU.max).then_inc(q2["ready"], 1)
                for c in range(NC):
                    k0, n = chunk(c)
                    dve.wait_ge(q2["done"], c + 1)
                    nc.vector.tensor_tensor(tab[:, k0:k0 + n, :], product(c), over(bmsg_s[:, 0, :], n),
                                            ALU.add).then_inc(q2["final"], 1)
                first_windows()

            @block.scalar
            def _(act):
                act.wait_ge(s_sq2, 1)
                nc.scalar.activation(stat[:, 2, :], stat[:, 2, :], ACT.Sqrt).then_inc(s_sqd2, 1)
                act_sweep(act, q2, False)

            @block.tensor
            def _(pe):
                pe.wait_ge(q2["ready"], NC)
                zero_sums()
                pe_sweep(pe, q2, cat[:, :, 0:D], top_s[:, 0, :], False)

        def gather_sums(q):
            for c in range(NC):
                k0, n = chunk(c)
                nc.vector.tensor_copy(cat[:, k0:k0 + n, D:2 * D], agg_chunk(c)).then_inc(q["ready"], 1)

        def apply_chunk(dve, chain, q, layer, c, to):
            k0, n = chunk(c)
            dve.wait_ge(q["done"], c + 1)
            w = work[:, k0:k0 + n, :]
            chain(nc.vector.tensor_tensor(w, product(c), over(bapp_s[:, layer, :], n), ALU.add))
            return nc.vector.scalar_tensor_tensor(to, w, 0.0, cat[:, k0:k0 + n, 0:D], ALU.max, ALU.add)

        sum_over_edges(tables[2], 0)
        q3, q4 = node_sems("app1"), node_sems("msg2")
        with nc.Block() as block:
            @block.sync
            def _(sp):
                clear_edge_sems(sp)
                store_table(sp, q4, tables[3])

            @block.gpsimd
            def _(pool):
                clear_gather_sems(pool)

            @block.vector
            def _(dve):
                chain = Chain(dve, q3["dve"])
                gather_sums(q3)
                for c in range(NC):
                    k0, n = chunk(c)
                    apply_chunk(dve, chain, q3, 0, c, cat[:, k0:k0 + n, 0:D]).then_inc(q3["final"], 1)
                for c in range(NC):
                    k0, n = chunk(c)
                    dve.wait_ge(q4["done"], c + 1)
                    nc.vector.tensor_tensor(tab[:, k0:k0 + n, :], product(c), over(bmsg_s[:, 1, :], n),
                                            ALU.add).then_inc(q4["final"], 1)
                first_windows()

            @block.scalar
            def _(act):
                act_sweep(act, q3, True)
                act_sweep(act, q4, False)

            @block.tensor
            def _(pe):
                pe.wait_ge(q3["ready"], NC)
                zero_sums()
                pe_sweep(pe, q3, cat, app_s[:, 0, :], True)
                pe_sweep(pe, dict(q4, ready=q3["final"]), cat[:, :, 0:D], top_s[:, 1, :], False, before=q3)

        sum_over_edges(tables[3], 1)
        q5 = node_sems("app2")
        with nc.Block() as block:
            @block.sync
            def _(sp):
                for c in range(NC):
                    k0, n = chunk(c)
                    sp.wait_ge(q5["final"], c + 1)
                    if c < NC - 1:
                        sp.dma_start(out[k0 * P:(k0 + n) * P, :].rearrange("(k p) d -> p k d", p=P),
                                     work[:, k0:k0 + n, :]).then_inc(q5["out"], 16)
                    else:
                        sp.dma_start(out[k0 * P:N, :], work[0:NTAIL, k0, :]).then_inc(q5["out"], 16)
                sp.wait_ge(q5["out"], 16 * NC)

            @block.vector
            def _(dve):
                chain = Chain(dve, q5["dve"])
                gather_sums(q5)
                for c in range(NC):
                    k0, n = chunk(c)
                    w = work[:, k0:k0 + n, :]
                    chain(apply_chunk(dve, chain, q5, 1, c, w))
                    nc.vector.tensor_tensor(w, w, xs[:, k0:k0 + n, :], ALU.add).then_inc(q5["final"], 1)

            @block.scalar
            def _(act):
                act_sweep(act, q5, True)

            @block.tensor
            def _(pe):
                pe_sweep(pe, q5, cat, app_s[:, 1, :], True)


_INS = ['x', 'src', 'dst', 'edge_attr_64', 'L0_gnn_W1', 'L0_gnn_b1', 'L0_gnn_W2', 'L0_gnn_b2',
        'L1_gnn_W1_msg', 'L1_gnn_b1_msg', 'L1_gnn_W1_app', 'L1_gnn_b1_app',
        'L1_gnn_W2_msg', 'L1_gnn_b2_msg', 'L1_gnn_W2_app', 'L1_gnn_b2_app']
_OUT = (3125, 64)


def kernel(**inputs):
    import numpy as _np
    import concourse.bacc as _bacc
    from concourse import mybir as _mybir
    from concourse.bass_utils import run_bass_kernel_spmd as _run

    nc = _bacc.Bacc("TRN2", target_bir_lowering=False, num_devices=1)
    arrays, args = {}, []
    for name in _INS:
        a = _np.ascontiguousarray(inputs[name])
        arrays[f"in_{name}_dram"] = a
        args.append(nc.dram_tensor(f"in_{name}_dram", a.shape, _mybir.dt.from_np(a.dtype), kind="ExternalInput").ap())
    args.append(nc.dram_tensor("out_0_dram", _OUT, _mybir.dt.float32, kind="ExternalOutput").ap())
    gnn_kernel(nc, *args)
    r = _run(nc, [arrays], core_ids=[0])
    return r.results[0]["out_0_dram"]
```

```python
import concourse.bass as bass
from concourse import mybir
from contextlib import ExitStack

P = 128
N = 3125
E = 53125
D = 64
MID = 128
NB = -(-N // P)
NTAIL = N - (NB - 1) * P
AGGB = NB + 1
TPG = 8
GE = P * TPG
NG = -(-E // GE)
ETAIL = E - (NG - 1) * GE
TFULL = ETAIL // TPG
TREST = ETAIL - TFULL * TPG
R = 4
NIT = NG // R
WIN = 2 * P
SHIFTS = -(-NB // 2) - 1
HALF = P // 2
NO_NODE = 1 << 20
DW = 72
DPB = 512 // DW
DBANKS = -(-NB // DPB)
GATHERED = (32, 20)
MADE_PER_TURN = 2
KEPT_PER_TURN = 4
HOTW = WIN + 2
KEPT = NG - GATHERED[0]
ND = NG - GATHERED[1]
CB = 4
NC = -(-NB // CB)
EPS = 1e-5

fp32 = mybir.dt.float32
bf16 = mybir.dt.bfloat16
fp16 = mybir.dt.float16
i32 = mybir.dt.int32
ALU = mybir.AluOpType
ACT = mybir.ActivationFunctionType
AX = mybir.AxisListType


def chunk(c):
    return c * CB, min(CB, NB - c * CB)


class Chain:

    def __init__(self, engine, sem):
        self.engine, self.sem, self.n = engine, sem, 0

    def __call__(self, ins):
        self.n += 1
        ins.then_inc(self.sem, 1)
        self.engine.wait_ge(self.sem, self.n)


def gnn_kernel(nc, x, src, dst, efeat, W1, b1, W2, b2,
               W1_msg, b1_msg, W1_app, b1_app, W2_msg, b2_msg, W2_app, b2_app, out):
    ctx = ExitStack()
    with ctx:
        def sb(name, shape, dt=fp32):
            return ctx.enter_context(nc.sbuf_tensor(name, shape, dt))

        def sem(name):
            return ctx.enter_context(nc.semaphore(name))

        tables = [nc.dram_tensor(f"table{i}", (P * NB, 3 * D if i < 2 else D), bf16 if i < 2 else fp32).ap()
                  for i in range(4)]
        kept = nc.dram_tensor("kept", (KEPT, P, NB * DW), fp16).ap()

        src_i = sb("src_i", [P, NG, TPG], i32)
        dst_i = sb("dst_i", [P, NG, TPG], i32)
        tmp_i = sb("tmp_i", [P, NG, TPG], i32)
        row_i = sb("row_i", [P, NG + R, TPG], i32)
        dst_lo = sb("dst_lo", [P, NG, TPG])
        dst_hi = sb("dst_hi", [P, NG, TPG])
        dst_f = sb("dst_f", [P, NG, TPG])
        rel0 = sb("rel0", [P, NG, TPG])
        rel = sb("rel", [P, NG, TPG])
        outside = sb("outside", [P, NG, TPG])
        src_lo = sb("src_lo", [P, ND, TPG])
        pair = sb("pair", [P, ND, TPG])
        pair_in = sb("pair_in", [P, ND, TPG])
        gmin = sb("gmin", [P, NG])
        bmin = sb("bmin", [NG, 2])
        bmin_i = sb("bmin_i", [NG, 1], i32)
        bdiag = sb("bdiag", [NG, 2 * NG])
        base = sb("base", [P, NG])
        first = sb("first", [P, NG])
        offset = sb("offset", [P, NG])
        col0 = sb("col0", [1, NG], i32)
        col = sb("col", [1, NG], i32)
        far = sb("far", [P, 1])
        farT = sb("farT", [1, 1])
        flag = sb("flag", [1, 1], i32)
        idx = sb("idx", [P, R, TPG], i32)
        rows_mem = sb("rows_mem", [P, R * TPG * 3 * D // 2])
        rows3 = rows_mem[:, :].bitcast(bf16).rearrange("p (r n) -> p r n", r=R)
        rows = rows_mem[:, 0:R * TPG * D].rearrange("p (r n) -> p r n", r=R)
        late_mem = sb("late_mem", [P, NB * 2 * D + R * TPG * D + 8 * P + 5 * TPG * D])
        at = NB * 2 * D
        cat = late_mem[:, 0:at].rearrange("p (k d) -> p k d", k=NB)
        ef = late_mem[:, at:at + R * TPG * D].rearrange("p (r n) -> p r n", r=R)
        at += R * TPG * D
        efT = late_mem[:, at:at + 8 * P].rearrange("p (r n) -> p r n", r=2)
        at += 8 * P
        msg = late_mem[:, at:at + 2 * TPG * D].rearrange("p (r n) -> p r n", r=2)
        at += 2 * TPG * D
        msg3 = late_mem[:, at:at + 3 * TPG * D].bitcast(bf16).rearrange("p (r a n) -> p r a n", r=2, a=3)
        counts = sb("counts", [P, 4, NB * DW], fp16)
        parts = sb("parts", [P, NB, 3, D], bf16)
        dsum = sb("dsum", [DW, D])
        place = sb("place", [DW, WIN])
        diag_i = sb("diag_i", [P, WIN], i32)
        diag_f = sb("diag_f", [P, WIN])
        onehot = sb("onehot", [P, 2, TPG, HOTW], bf16)
        iota_i = sb("iota_i", [P, HOTW], i32)
        iota_f = sb("iota_f", [P, P])
        iota3 = sb("iota3", [P, 3, HOTW // 3 + 2], bf16)
        part_i = sb("part_i", [P, 1], i32)
        part_f = sb("part_f", [P, 1])
        ident = sb("ident", [P, P])
        zeros_b = sb("zeros_b", [P, 512], bf16)
        ones = sb("ones", [P, P])
        pool_mem = sb("pool_mem", [P, 7716])
        catT = pool_mem[:, 0:NB * P]
        midT = pool_mem[:, NB * P:2 * NB * P]
        pool16 = pool_mem[:, :].bitcast(bf16)
        hot_lo = pool16[:, 0:2 * TPG * HALF].rearrange("p (b t n) -> p b t n", b=2, t=TPG)
        hot_hi = pool16[:, 2 * TPG * HALF:2 * TPG * (HALF + 2 * NB)].rearrange("p (b t n) -> p b t n", b=2, t=TPG)
        hot_mem = [m[:, 0:TPG * (NB * DW + P + 1) // 2].bitcast(fp16) for m in (pool_mem, late_mem)]
        hot_pair = [m[:, 0:TPG * NB * DW].rearrange("p (t n) -> p t n", t=TPG) for m in hot_mem]
        hot_src = [m[:, TPG * NB * DW:TPG * (NB * DW + P + 1)].rearrange("p (t n) -> p t n", t=TPG) for m in hot_mem]
        iota_h = sb("iota_h", [P, NB, DW + 8], fp16)
        iota_s = sb("iota_s", [P, 3, 46], fp16)
        dis = sb("dis", [P, NB])
        xs = sb("xs", [P, NB, D])
        tab = sb("tab", [P, NB, D])
        work = sb("work", [P, NB, D])
        stat = sb("stat", [P, 4, NB])
        eps = sb("eps", [P, 1])
        W1_s = sb("W1_s", [D, MID])
        W2_s = sb("W2_s", [MID, D])
        b1_s = sb("b1_s", [MID, 1])
        b2_s = sb("b2_s", [P, D])
        top_s = sb("top_s", [D, 2, D])
        bot_s = sb("bot_s", [P, 2, P])
        app_s = sb("app_s", [P, 2, D])
        bmsg_s = sb("bmsg_s", [P, 2, D])
        bapp_s = sb("bapp_s", [P, 2, D])

        agg = ctx.enter_context(nc.psum_tensor("agg", [P, 2048], fp32))
        tp = ctx.enter_context(nc.psum_tensor("tp", [P, 2, 512], fp32))
        mm = ctx.enter_context(nc.psum_tensor("mm", [P, 2, 512], fp32))

        def agg_chunk(c):
            k, n = chunk(c)
            return agg[:, k * D:(k + n) * D].rearrange("p (k d) -> p k d", d=D)

        staged = sem("staged")
        started = sem("started")
        gathered = [sem(f"gathered{j}") for j in range(R)]
        loaded = [sem(f"loaded{j}") for j in range(R)]
        hot_ready = sem("hot_ready")
        summed = sem("summed")
        turned = sem("turned")
        copied = sem("copied")
        projected = sem("projected")
        added = sem("added")
        term1 = sem("term1")
        rest = sem("rest")
        term2 = sem("term2")
        msg_ready = sem("msg_ready")
        edge_sems = [staged, started, *loaded, hot_ready, summed, turned, copied, projected, added, term1, rest, term2,
                     msg_ready]
        pair_ready = sem("pair_ready")
        bank_full = sem("bank_full")
        bank_copied = sem("bank_copied")
        stored = [sem(f"stored{u}") for u in range(2)]
        reloaded = [sem(f"reloaded{u}") for u in range(2)]
        applied = sem("applied")
        reduced = sem("reduced")
        placed = sem("placed")
        edge_sems += [pair_ready, bank_full, bank_copied, *stored, *reloaded, applied, reduced, placed]

        def edge_pass(table, layer):
            with nc.Block() as block:
                @block.gpsimd
                def _(pool):
                    with pool.Fori(0, NIT) as it:
                        for j in range(R):
                            pool.wait_ge(staged, it * R + (j + 1))
                            pool.sem_inc(started, 1)
                            for t in range(TPG):
                                nc.gpsimd.indirect_dma_start(
                                    out=(rows3[:, j, 3 * t * D:3 * (t + 1) * D] if layer is None else
                                         rows[:, j, t * D:(t + 1) * D]), out_offset=None, in_=table[:, :],
                                    in_offset=bass.IndirectOffsetOnAxis(ap=idx[:, j, t:t + 1], axis=0),
                                ).then_inc(gathered[j], 16)
                    for j in range(R):
                        pool.wait_ge(gathered[j], NIT * TPG * 16)

                @block.sync
                def _(sp):
                    if layer is None:
                        return

                    def load(g, j):
                        sp.dma_start(ef[:, j, :], efeat[bass.ds(g * GE, GE), :].rearrange(
                            "(p t) f -> p (t f)", t=TPG)).then_inc(loaded[j], 16)

                    for j in range(R):
                        load(j, j)
                    with sp.Fori(1, NIT - 1) as it:
                        for j in range(R):
                            sp.wait_ge(turned, (it - 1) * R + (j + 1))
                            load(it * R + j, j)
                    for j in range(R):
                        sp.wait_ge(turned, (NIT - 2) * R + j + 1)
                        if j < R - 1:
                            load((NIT - 1) * R + j, j)
                    e0 = (NG - 1) * GE
                    sp.dma_start(ef[0:TFULL, R - 1, :], efeat[e0:e0 + TFULL * TPG, :].rearrange(
                        "(p t) f -> p (t f)", t=TPG)).then_inc(loaded[R - 1], 16)
                    sp.dma_start(ef[TFULL:TFULL + 1, R - 1, 0:TREST * D], efeat[E - TREST:E, :].rearrange(
                        "(p t) f -> p (t f)", t=TREST)).then_inc(loaded[R - 1], 16)

                @block.vector
                def _(dve):
                    def stage(g, j):
                        nc.vector.tensor_copy(idx[:, j:j + 1, :], row_i[:, bass.ds(g, 1), :]).then_inc(staged, 1)

                    def one_hot(g, j):
                        for t in range(TPG):
                            last = nc.vector.tensor_scalar(
                                onehot[:, j % 2, t, :], iota3[:, :, 0:HOTW // 3], rel[:, bass.ds(g, 1), t:t + 1].rearrange("p a b -> p (a b)"),
                                None, ALU.is_equal)
                        last.then_inc(hot_ready, 1)

                    def step(g, j, first):
                        if first and j < 2:
                            one_hot(g, j)
                        else:
                            dve.wait_ge(summed, g - 1)
                            one_hot(g, j)
                        if layer is None:
                            if not (first and j == 0):
                                dve.wait_ge(summed, g)
                                stage(g + (R - 1), (j - 1) % R)
                        else:
                            dve.wait_ge(projected, g + 1)
                            dve.wait_ge(gathered[j], (g - j) * (TPG * 16 // R) + TPG * 16)
                            nc.vector.tensor_tensor(msg[:, j % 2, :], mm[:, j % 2, :], rows[:, j, :],
                                                    ALU.add).then_inc(added, 1)
                            dve.wait_ge(added, g + 1)
                            stage(g + R, j)
                            dve.wait_ge(term1, g + 1)
                            nc.vector.scalar_tensor_tensor(msg[:, j % 2, :], msg[:, j % 2, :], 0.0,
                                                           msg3[:, j % 2, 0, :], ALU.max, ALU.subtract).then_inc(rest, 1)
                            dve.wait_ge(term2, g + 1)
                            nc.vector.tensor_tensor(msg3[:, j % 2, 2, :], msg[:, j % 2, :], msg3[:, j % 2, 1, :],
                                                    ALU.subtract).then_inc(msg_ready, 1)

                    for j in range(R):
                        stage(j, j)
                    for j in range(R):
                        step(j, j, True)
                    with dve.Fori(1, NIT) as it:
                        for j in range(R):
                            step(it * R + j, j, False)

                @block.scalar
                def _(act):
                    if layer is None:
                        return

                    def copy(g, b):
                        act.wait_ge(turned, g + 1)
                        nc.scalar.copy(efT[:, b, :], tp[:, 0, :]).then_inc(copied, 1)

                    def relu(g, b):
                        act.wait_ge(added, g + 1)
                        nc.scalar.activation(msg3[:, b, 0, :], msg[:, b, :], ACT.Relu).then_inc(term1, 1)
                        act.wait_ge(rest, g + 1)
                        nc.scalar.copy(msg3[:, b, 1, :], msg[:, b, :]).then_inc(term2, 1)

                    copy(0, 0)
                    with act.Fori(0, NIT - 1) as it:
                        for j in range(R):
                            copy(it * R + (j + 1), (j + 1) % 2)
                            relu(it * R + j, j % 2)
                    for j in range(R):
                        g = (NIT - 1) * R + j
                        if g + 1 < NG:
                            copy(g + 1, (j + 1) % 2)
                        relu(g, j % 2)

                @block.tensor
                def _(pe):
                    def turn(g, j, count):
                        pe.wait_ge(loaded[j], count)
                        for q in range(TPG // 2):
                            last = nc.tensor.transpose(tp[:, 0, q * P:(q + 1) * P],
                                                       ef[:, j, q * P:(q + 1) * P], ident[:])
                        last.then_inc(turned, 1)

                    def project(g, j):
                        pe.wait_ge(copied, g + 1)
                        for q in range(TPG // 2):
                            last = nc.tensor.matmul(mm[:, j % 2, q * P:(q + 1) * P],
                                                    lhsT=efT[:, j % 2, q * P:(q + 1) * P], rhs=bot_s[:, layer, :],
                                                    start=True, stop=True)
                        last.then_inc(projected, 1)

                    def scatter(g, j, at):
                        pe.wait_ge(hot_ready, g + 1)
                        if layer is None:
                            pe.wait_ge(gathered[j], (g - j) * (TPG * 16 // R) + TPG * 16)
                        else:
                            pe.wait_ge(msg_ready, g + 1)
                        for w in range(2):
                            sums = agg[:, bass.ds(at + w * D, D)]
                            for t in range(TPG):
                                for a in range(3):
                                    term = (rows3[:, j, (3 * t + a) * D:(3 * t + a + 1) * D] if layer is None else
                                            msg3[:, j % 2, a, t * D:(t + 1) * D])
                                    last = nc.tensor.matmul(sums, lhsT=onehot[:, j % 2, t, w * P:(w + 1) * P], rhs=term,
                                                            start=False, stop=True, skip_group_check=True)
                        last.then_inc(summed, 1)

                    def columns(g0):
                        return [pe.value_load(col[0:1, bass.ds(g0 + j, 1)], min_val=0, max_val=(NB - 1) * D)
                                for j in range(R)]

                    if layer is None:
                        with pe.Fori(0, NIT) as it:
                            at = columns(it * R)
                            for j in range(R):
                                scatter(it * R + j, j, at[j])
                        return
                    turn(0, 0, 16)
                    project(0, 0)
                    with pe.Fori(0, NIT - 1) as it:
                        at = columns(it * R)
                        for j in range(R):
                            n = (j + 1) % R
                            turn(it * R + (j + 1), n, it * 16 + (16 if j < R - 1 else 32))
                            scatter(it * R + j, j, at[j])
                            project(it * R + (j + 1), n)
                    at = columns((NIT - 1) * R)
                    for j in range(R):
                        g = (NIT - 1) * R + j
                        if g + 1 < NG:
                            turn(g + 1, j + 1, NIT * 16 + (16 if g + 1 == NG - 1 else 0))
                        scatter(g, j, at[j])
                        if g + 1 < NG:
                            project(g + 1, j + 1)

        def convolution_pass(table, which):
            ng = GATHERED[which]
            turns = ng // R
            made = NG - ng if which == 0 else ND - KEPT
            early = made - MADE_PER_TURN * turns
            per_turn = KEPT_PER_TURN if which else 0
            in_turn = MADE_PER_TURN + per_turn
            assert early % 2 == 0 and KEPT_PER_TURN * (GATHERED[1] // R) == KEPT
            d0 = ng - GATHERED[1]

            with nc.Block() as block:
                @block.gpsimd
                def _(pool):
                    with pool.Fori(0, turns) as it:
                        for j in range(R):
                            pool.wait_ge(staged, it * R + (j + 1))
                            pool.sem_inc(started, 1)
                            for t in range(TPG):
                                nc.gpsimd.indirect_dma_start(
                                    out=rows3[:, j, 3 * t * D:3 * (t + 1) * D], out_offset=None, in_=table[:, :],
                                    in_offset=bass.IndirectOffsetOnAxis(ap=idx[:, j, t:t + 1], axis=0),
                                ).then_inc(gathered[j], 16)
                    for j in range(R):
                        pool.wait_ge(gathered[j], turns * TPG * 16)

                @block.sync
                def _(sp):
                    def keep(i, slot):
                        sp.wait_ge(bank_copied, (i + 1) * DBANKS)
                        sp.dma_start(kept[bass.ds(i, 1), :, :].rearrange("a p n -> p (a n)"), counts[:, slot, :]
                                     ).then_inc(stored[slot], 16)

                    def reload(r, slot, k):
                        sp.wait_ge(applied, k)
                        sp.dma_start(counts[:, 2 + slot, :], kept[bass.ds(r, 1), :, :].rearrange("a p n -> p (a n)")
                                     ).then_inc(reloaded[slot], 16)

                    if which == 0:
                        for i in range(early):
                            keep(i, i % 2)
                        with sp.Fori(0, turns) as it:
                            for h in range(2):
                                keep(it * 2 + (early + h), h)
                        for u in range(2):
                            sp.wait_ge(stored[u], 16 * made // 2)
                    else:
                        with sp.Fori(0, turns) as it:
                            for h in range(2):
                                for u in range(2):
                                    reload(it * per_turn + (2 * h + u), u, it * in_turn + (early + 3 * h + u - 1))

                @block.vector
                def _(dve):
                    def stage(g, j):
                        nc.vector.tensor_copy(idx[:, j:j + 1, :], row_i[:, bass.ds(g, 1), :]).then_inc(staged, 1)

                    def one_hot(g, j):
                        for t in range(TPG):
                            last = nc.vector.tensor_scalar(
                                onehot[:, j % 2, t, :], iota3[:, :, 0:HOTW // 3], rel[:, bass.ds(g, 1), t:t + 1].rearrange("p a b -> p (a b)"),
                                None, ALU.is_equal)
                        last.then_inc(hot_ready, 1)

                    def pair_hot(i, b, t0, t1):
                        for t in range(t0, t1):
                            nc.vector.tensor_scalar(
                                hot_src[b][:, t, :], iota_s[:, :, 0:(P + 1) // 3],
                                src_lo[:, bass.ds(d0 + i, 1), t:t + 1].rearrange("p a b -> p (a b)"), None, ALU.is_equal)
                            last = nc.vector.tensor_scalar(
                                hot_pair[b][:, t, :], iota_h[:, :, 0:DW],
                                pair[:, bass.ds(d0 + i, 1), t:t + 1].rearrange("p a b -> p (a b)"), None, ALU.is_equal)
                        if t1 == TPG:
                            last.then_inc(pair_ready, 1)

                    def reduce(k, g, started_before=True):
                        if started_before:
                            dve.wait_ge(placed, k)
                        nc.vector.tensor_scalar(place[:], diag_f[0:DW, :], offset[0:DW, bass.ds(g, 1)], None, ALU.is_equal)
                        dve.wait_ge(applied, k + 1)
                        nc.vector.tensor_reduce(dsum[:], tp[0:DW, 0, 0:3 * D].rearrange("p (a d) -> p d a", a=3),
                                                AX.X, ALU.add).then_inc(reduced, 1)

                    for j in range(R):
                        stage(j, j)
                    pair_hot(0, 0, 0, TPG)
                    for i in range(early):
                        if i:
                            dve.wait_ge(bank_full, DBANKS * i)
                        pair_hot(i + 1, (i + 1) % 2, 0, TPG)
                        reduce(i, ng + i, i > 0)

                    def turn(it, first, last):
                        for h in range(2):
                            g = it * R + 2 * h
                            i = it * MADE_PER_TURN + (early + h)
                            k = it * in_turn + (early + h * in_turn // 2)
                            if not (first and h == 0):
                                dve.wait_ge(summed, g)
                                stage(g + 2, (2 * h + 2) % R)
                                stage(g + 3, (2 * h + 3) % R)
                            one_hot(g, 2 * h)
                            one_hot(g + 1, 2 * h + 1)
                            more = not (last and h == 1)
                            if more:
                                dve.wait_ge(bank_full, i * DBANKS)
                                pair_hot(i + 1, 1 - h, 0, 4)
                            reduce(k, i + ng)
                            for u in range(per_turn // 2):
                                if more:
                                    pair_hot(i + 1, 1 - h, 4 + 2 * u, 6 + 2 * u)
                                reduce(k + (1 + u), it * per_turn + (GATHERED[0] + h * per_turn // 2 + u))
                            if more and not per_turn:
                                pair_hot(i + 1, 1 - h, 4, TPG)

                    turn(0, True, False)
                    with dve.Fori(1, turns - 1) as it:
                        turn(it, False, False)
                    turn(turns - 1, False, True)

                @block.scalar
                def _(act):
                    def copy_counts(i, slot, before):
                        if which == 0 and before is not None:
                            act.wait_ge(stored[slot], before * 16)
                        for b in range(DBANKS):
                            n = min(DPB, NB - b * DPB) * DW
                            act.wait_ge(bank_full, i * DBANKS + (b + 1))
                            nc.scalar.copy(counts[:, slot, b * DPB * DW:b * DPB * DW + n], mm[:, b % 2, 0:n]).then_inc(
                                bank_copied, 1)

                    for i in range(early):
                        copy_counts(i, i % 2, i // 2 or None)
                    with act.Fori(0, turns) as it:
                        for h in range(2):
                            copy_counts(it * MADE_PER_TURN + (early + h), h, it + early // 2)

                @block.tensor
                def _(pe):
                    def scatter(g, j, at):
                        pe.wait_ge(hot_ready, g + 1)
                        pe.wait_ge(gathered[j], (g - j) * (TPG * 16 // R) + TPG * 16)
                        for w in range(2):
                            sums = agg[:, bass.ds(at + w * D, D)]
                            for t in range(TPG):
                                for a in range(3):
                                    last = nc.tensor.matmul(sums, lhsT=onehot[:, j % 2, t, w * P:(w + 1) * P],
                                                            rhs=rows3[:, j, (3 * t + a) * D:(3 * t + a + 1) * D],
                                                            start=False, stop=True, skip_group_check=True)
                        last.then_inc(summed, 1)

                    def count(i, slot):
                        pe.wait_ge(pair_ready, i + 1)
                        for b in range(DBANKS):
                            n = min(DPB, NB - b * DPB) * DW
                            if b >= 2:
                                pe.wait_ge(bank_copied, i * DBANKS + (b - 1))
                            for t in range(TPG):
                                last = nc.tensor.matmul(mm[:, b % 2, 0:n], lhsT=hot_src[slot][:, t, 0:P],
                                                        rhs=hot_pair[slot][:, t, b * DPB * DW:b * DPB * DW + n],
                                                        start=(t == 0), stop=(t == TPG - 1))
                            last.then_inc(bank_full, 1)

                    def apply(slot):
                        for k in range(NB):
                            last = nc.tensor.matmul(tp[0:DW, 0, 0:3 * D], lhsT=counts[:, slot, k * DW:(k + 1) * DW],
                                                    rhs=parts[:, k, :, :].rearrange("p a d -> p (a d)"),
                                                    start=(k == 0), stop=(k == NB - 1))
                        last.then_inc(applied, 1)

                    def put(k, at):
                        pe.wait_ge(reduced, k + 1)
                        for w in range(2):
                            last = nc.tensor.matmul(agg[:, bass.ds(at + w * D, D)], lhsT=place[:, w * P:(w + 1) * P],
                                                    rhs=dsum[:], start=False, stop=True, skip_group_check=True)
                        last.then_inc(placed, 1)

                    def column(g):
                        return pe.value_load(col[0:1, bass.ds(g, 1)], min_val=0, max_val=(NB - 1) * D)

                    def made(i, slot):
                        pe.wait_ge(bank_copied, (i + 1) * DBANKS)
                        apply(slot)

                    for i in range(early):
                        count(i, i % 2)
                        made(i, i % 2)
                        put(i, column(ng + i))
                    with pe.Fori(0, turns) as it:
                        for h in range(2):
                            g = it * R + 2 * h
                            i = it * MADE_PER_TURN + (early + h)
                            k = it * in_turn + (early + h * in_turn // 2)
                            r = it * per_turn + h * per_turn // 2
                            at = [column(g), column(g + 1), column(i + ng)]
                            old = [column(r + (GATHERED[0] + u)) for u in range(per_turn // 2)]
                            count(i, h)
                            made(i, h)
                            scatter(g, 2 * h, at[0])
                            put(k, at[2])
                            if per_turn:
                                pe.wait_ge(reloaded[0], it * 32 + 16 * (h + 1))
                                apply(2)
                            scatter(g + 1, 2 * h + 1, at[1])
                            if per_turn:
                                put(k + 1, old[0])
                                pe.wait_ge(reloaded[1], it * 32 + 16 * (h + 1))
                                apply(3)
                                put(k + 2, old[1])

        def zero_sums():
            for b in range(0, AGGB * D, 512):
                n = min(512, AGGB * D - b)
                last = nc.tensor.matmul(agg[:, b:b + n], lhsT=zeros_b[:, 0:P], rhs=zeros_b[:, 0:n],
                                        start=True, stop=True, skip_group_check=True)
            return last

        def clear_edge_sems(sp):
            for s in edge_sems:
                sp.sem_clear(s)

        def clear_gather_sems(pool):
            pool.dma_reset(range(gathered[0].num, gathered[-1].num + 1))
            for s in gathered:
                pool.sem_clear(s)

        s_shift = sem("s_shift")

        def shift_windows():
            with nc.Block() as block:
                @block.sync
                def _(sp):
                    clear_edge_sems(sp)

                @block.gpsimd
                def _(pool):
                    clear_gather_sems(pool)

                @block.vector
                def _(dve):
                    nc.vector.tensor_scalar(rel[:], rel[:], float(-WIN), None, ALU.add)
                    nc.vector.tensor_scalar(col[:], col[:], 2 * D, (NB - 1) * D, ALU.add, ALU.min)

        def convolve(table, which):
            outlying = nc.values_load(flag[0:1, 0:1], min_val=0, max_val=1)
            with nc.If(outlying < 1):
                convolution_pass(table, which)
            with nc.Else():
                edge_pass(table, None)
                with nc.Fori(0, SHIFTS):
                    shift_windows()
                    edge_pass(table, None)

        def sum_over_edges(table, layer):
            edge_pass(table, layer)
            outlying = nc.values_load(flag[0:1, 0:1], min_val=0, max_val=1)
            with nc.If(outlying > 0):
                with nc.Fori(0, SHIFTS):
                    shift_windows()
                    edge_pass(table, layer)

        def bcast(ap, n):
            return ap.unsqueeze(2).to_broadcast([P, ap.shape[1], n])

        def layer_norm(dve, chain, s_sqrt_in, s_sqrt_out):
            mean, var, std, rstd = (stat[:, i, :] for i in range(4))
            chain(nc.vector.tensor_reduce(mean, xs[:], AX.X, ALU.add))
            chain(nc.vector.tensor_scalar(mean, mean, 1.0 / D, None, ALU.mult))
            chain(nc.vector.tensor_tensor(work[:], xs[:], bcast(mean, D), ALU.subtract))
            chain(nc.vector.tensor_tensor(tab[:], work[:], work[:], ALU.mult))
            chain(nc.vector.tensor_reduce(var, tab[:], AX.X, ALU.add))
            chain(nc.vector.tensor_scalar(var, var, 1.0 / D, EPS, ALU.mult, ALU.add))
            nc.vector.tensor_copy(std, var).then_inc(s_sqrt_in, 1)
            dve.wait_ge(s_sqrt_out, 1)
            chain(nc.vector.reciprocal(rstd, std))
            chain(nc.vector.tensor_tensor(work[:], work[:], bcast(rstd, D), ALU.mult))

        def node_sems(name):
            return {k: sem(f"{name}_{k}") for k in ("dve", "ready", "turned", "copied", "mid", "relu", "done", "rows", "term1", "rest", "term2",
                                                  "final", "out")}

        def split_dve(dve, q, c):
            if 1 <= c <= NC:
                k0, n = chunk(c - 1)
                dve.wait_ge(q["term1"], c)
                nc.vector.tensor_tensor(work[:, k0:k0 + n, :], tab[:, k0:k0 + n, :], parts[:, k0:k0 + n, 0, :],
                                        ALU.subtract).then_inc(q["rest"], 1)
            if c >= 2:
                k0, n = chunk(c - 2)
                dve.wait_ge(q["term2"], c - 1)
                nc.vector.tensor_tensor(parts[:, k0:k0 + n, 2, :], work[:, k0:k0 + n, :], parts[:, k0:k0 + n, 1, :],
                                        ALU.subtract).then_inc(q["final"], 1)

        def split_act(act, q, c):
            if c < NC:
                k0, n = chunk(c)
                act.wait_ge(q["rows"], c + 1)
                nc.scalar.copy(parts[:, k0:k0 + n, 0, :], tab[:, k0:k0 + n, :]).then_inc(q["term1"], 1)
            if 1 <= c <= NC:
                k0, n = chunk(c - 1)
                act.wait_ge(q["rest"], c)
                nc.scalar.copy(parts[:, k0:k0 + n, 1, :], work[:, k0:k0 + n, :]).then_inc(q["term2"], 1)

        s_dst = sem("s_dst"); s_src = sem("s_src"); s_x = sem("s_x"); s_w = sem("s_w"); s_fill = sem("s_fill"); s_io = sem("s_io")
        s_dve = sem("s_dve"); s_sq = sem("s_sq"); s_sqd = sem("s_sqd")
        s_hot = sem("s_hot"); s_deg = sem("s_deg"); s_const = sem("s_const");
        s_gm = sem("s_gm"); s_gt = sem("s_gt"); s_bd = sem("s_bd"); s_bb = sem("s_bb")
        s_far = sem("s_far"); s_ft = sem("s_ft");

        def bias_rows(b):
            return b.rearrange("(a n) -> a n", a=1).to_broadcast([P, D])

        def store_table(sp, q, table):
            view = table.rearrange("(p k) d -> p k d", k=NB)
            rows_ = parts[:, :, :, :].rearrange("p k a d -> p k (a d)") if table.shape[1] > D else tab
            for c in range(NC):
                k0, n = chunk(c)
                sp.wait_ge(q["final"], c + 1)
                sp.dma_start(view[:, k0:k0 + n, :], rows_[:, k0:k0 + n, :]).then_inc(q["out"], 16)
            sp.wait_ge(q["out"], 16 * NC)

        q0 = node_sems("first")
        with nc.Block() as block:
            @block.sync
            def _(sp):
                sp.wait_ge(s_fill, 1)
                for to, of, s_idx in ((dst_i, dst, s_dst), (src_i, src, s_src)):
                    full = (NG - 1) * GE
                    sp.dma_start(to[:, 0:NG - 1, :], of[0:full].rearrange("(g p t) -> p g t", p=P, t=TPG)
                                 ).then_inc(s_idx, 16)
                    sp.dma_start(to[0:TFULL, NG - 1:NG, :], of[full:full + TFULL * TPG].rearrange(
                        "(p g t) -> p g t", g=1, t=TPG)).then_inc(s_idx, 16)
                    sp.dma_start(to[TFULL:TFULL + 1, NG - 1:NG, 0:TREST], of[E - TREST:E].rearrange(
                        "(p g t) -> p g t", p=1, g=1)).then_inc(s_idx, 16)
                store_table(sp, q0, tables[0])

            @block.scalar
            def _(act):
                act.wait_ge(s_fill, 1)
                act.dma_start(xs[:, 0:NB - 1, :], x[0:(NB - 1) * P, :].rearrange("(k p) d -> p k d", p=P)
                              ).then_inc(s_x, 16)
                act.dma_start(xs[0:NTAIL, NB - 1, :], x[(NB - 1) * P:N, :]).then_inc(s_x, 16)
                act.dma_start(W1_s[:], W1).then_inc(s_w, 16)
                act.dma_start(W2_s[:], W2).then_inc(s_w, 16)
                act.dma_start(b1_s[:], b1.rearrange("(p a) -> p a", a=1)).then_inc(s_w, 16)
                act.dma_start(b2_s[:], bias_rows(b2)).then_inc(s_w, 16)
                for l, (wm, bm, wa, ba) in enumerate(((W1_msg, b1_msg, W1_app, b1_app),
                                                      (W2_msg, b2_msg, W2_app, b2_app))):
                    act.dma_start(top_s[:, l, :], wm[0:D, :]).then_inc(s_w, 16)
                    act.dma_start(bot_s[0:D, l, 0:D], wm[D:2 * D, :]).then_inc(s_w, 16)
                    act.dma_start(bot_s[D:P, l, D:P], wm[D:2 * D, :]).then_inc(s_w, 16)
                    act.dma_start(app_s[:, l, :], wa).then_inc(s_w, 16)
                    act.dma_start(bmsg_s[:, l, :], bias_rows(bm)).then_inc(s_w, 16)
                    act.dma_start(bapp_s[:, l, :], bias_rows(ba)).then_inc(s_w, 16)
                act.wait_ge(s_sq, 1)
                nc.scalar.activation(stat[:, 2, :], stat[:, 2, :], ACT.Sqrt).then_inc(s_sqd, 1)
                act.wait_ge(s_sq, 2)
                nc.scalar.activation(dis[:], dis[:], ACT.Sqrt).then_inc(s_sqd, 1)
                for c in range(NC + 1):
                    split_act(act, q0, c)
                act.wait_ge(s_w, 16 * 16)

            @block.gpsimd
            def _(pool):
                nc.gpsimd.iota(iota_i[:], [[1, HOTW]], base=0, channel_multiplier=0).then_inc(s_io, 1)
                nc.gpsimd.iota(part_i[:], [[1, 1]], base=0, channel_multiplier=1).then_inc(s_io, 1)
                nc.gpsimd.iota(diag_i[:], [[1, WIN]], base=0, channel_multiplier=-1).then_inc(s_io, 1)
                nc.gpsimd.iota(iota_h[:, :, 0:DW], [[DW, NB], [1, DW]], base=0, channel_multiplier=0,
                               allow_small_or_imprecise_dtypes=True).then_inc(s_io, 1)

            @block.vector
            def _(dve):
                chain = Chain(dve, s_dve)
                nc.vector.memset(src_i[:, NG - 1, :], 0)
                nc.vector.memset(dst_i[:, NG - 1, :], NO_NODE)
                nc.vector.memset(xs[:, NB - 1, :], 0.0)
                nc.vector.memset(bot_s[:], 0.0).then_inc(s_fill, 1)
                nc.vector.memset(row_i[:], 0)
                nc.vector.memset(zeros_b[:], 0.0)
                nc.vector.memset(ones[:], 1.0)
                dve.wait_ge(s_io, 4)
                nc.vector.tensor_copy(diag_f[:], diag_i[:])
                nc.vector.tensor_copy(iota_f[:], iota_i[:, 0:P])
                nc.vector.tensor_copy(iota3[:, :, 0:HOTW // 3], iota_i[:, 0:HOTW].rearrange("p (a n) -> p a n", a=3))
                nc.vector.tensor_copy(iota_s[:, :, 0:(P + 1) // 3], iota_i[:, 0:P + 1].rearrange("p (a n) -> p a n", a=3))
                chain(nc.vector.tensor_copy(part_f[:], part_i[:]))
                nc.vector.tensor_scalar(ident[:], iota_f[:, 0:P], part_f[:], None, ALU.is_equal).then_inc(s_const, 1)
                dve.wait_ge(s_dst, 48)
                nc.vector.tensor_copy(dst_f[:], dst_i[:])
                chain(nc.vector.tensor_scalar(tmp_i[:], dst_i[:], 6, None, ALU.arith_shift_right))
                nc.vector.tensor_copy(dst_hi[:], tmp_i[:])
                chain(nc.vector.tensor_scalar(dst_i[:], dst_i[:], HALF - 1, None, ALU.bitwise_and))
                chain(nc.vector.tensor_copy(dst_lo[:], dst_i[:]))

                def degree_hot(g, b):
                    for hot, width, of in ((hot_lo, HALF, dst_lo), (hot_hi, 2 * NB, dst_hi)):
                        last = nc.vector.tensor_tensor(
                            hot[:, b, :, :], iota_f[:, 0:width].unsqueeze(1).to_broadcast([P, TPG, width]),
                            of[:, bass.ds(g, 1), :].rearrange("p a t -> p (a t)").unsqueeze(2).to_broadcast(
                                [P, TPG, width]), ALU.is_equal)
                    last.then_inc(s_hot, 1)

                for g in range(2):
                    degree_hot(g, g)
                with dve.Fori(1, NG // 2) as it:
                    for b in range(2):
                        dve.wait_ge(s_deg, it * 2 + (b - 1))
                        degree_hot(it * 2 + b, b)
                dve.wait_ge(s_src, 48)
                chain(nc.vector.tensor_scalar(tmp_i[:], src_i[:], P - 1, None, ALU.bitwise_and))
                chain(nc.vector.tensor_copy(src_lo[:], tmp_i[:, NG - ND:NG, :]))
                chain(nc.vector.tensor_scalar(tmp_i[:], tmp_i[:], NB, None, ALU.mult))
                chain(nc.vector.tensor_scalar(src_i[:], src_i[:], 7, None, ALU.arith_shift_right))
                nc.vector.tensor_tensor(row_i[:, 0:NG, :], src_i[:], tmp_i[:], ALU.add)
                nc.vector.tensor_reduce(gmin[:], dst_f[:], AX.X, ALU.min).then_inc(s_gm, 1)
                dve.wait_ge(s_gt, 1)
                chain(nc.vector.tensor_reduce(bmin[:, 1:2], tp[0:NG, 0, 0:P], AX.X, ALU.min))
                chain(nc.vector.tensor_copy(bmin_i[:], bmin[:, 1:2]))
                chain(nc.vector.tensor_scalar(bmin_i[:], bmin_i[:], 7, None, ALU.arith_shift_right))
                chain(nc.vector.tensor_copy(bmin[:, 0:1], bmin_i[:]))
                nc.vector.tensor_scalar(bdiag[:, 0:NG], ident[0:NG, 0:NG], bmin[:, 0:1], None, ALU.mult)
                nc.vector.tensor_scalar(bdiag[:, NG:2 * NG], ident[0:NG, 0:NG], bmin[:, 1:2], None, ALU.mult
                                        ).then_inc(s_bd, 1)
                dve.wait_ge(s_bb, 1)
                nc.vector.tensor_scalar(base[:], mm[:, 1, 0:NG], float(P), None, ALU.mult)
                nc.vector.tensor_copy(first[:], mm[:, 1, NG:2 * NG])
                nc.vector.tensor_scalar(col0[:], mm[0:1, 1, 0:NG], float(D), None, ALU.mult)
                chain(nc.vector.tensor_scalar(col[:], mm[0:1, 1, 0:NG], float(D), None, ALU.mult))
                nc.vector.tensor_tensor(offset[:], first[:], base[:], ALU.subtract)
                chain(nc.vector.tensor_tensor(rel0[:], dst_f[:], bcast(base[:], TPG), ALU.subtract))
                nc.vector.tensor_copy(rel[:], rel0[:])
                chain(nc.vector.tensor_scalar(outside[:], dst_f[:], float(NO_NODE), None, ALU.is_lt))
                last_groups = slice(NG - ND, NG)
                chain(nc.vector.tensor_tensor(pair[:], dst_f[:, last_groups, :], bcast(first[:, last_groups], TPG),
                                              ALU.subtract))
                chain(nc.vector.scalar_tensor_tensor(pair_in[:], pair[:], float(DW), outside[:, last_groups, :],
                                                     ALU.is_ge, ALU.mult))
                chain(nc.vector.scalar_tensor_tensor(outside[:], rel0[:], float(WIN), outside[:], ALU.is_ge, ALU.mult))
                chain(nc.vector.tensor_tensor(outside[:, last_groups, :], outside[:, last_groups, :], pair_in[:], ALU.max))
                nc.vector.tensor_reduce(far[:], outside[:], AX.XY, ALU.max).then_inc(s_far, 1)
                chain(nc.vector.tensor_scalar(pair_in[:], pair[:], float(DW), 4096.0, ALU.is_ge, ALU.mult))
                chain(nc.vector.tensor_tensor(pair[:], pair[:], pair_in[:], ALU.add))
                chain(nc.vector.tensor_copy(pair_in[:], src_i[:, last_groups, :]))
                nc.vector.scalar_tensor_tensor(pair[:], pair_in[:], float(DW), pair[:], ALU.mult, ALU.add)
                dve.wait_ge(s_ft, 1)
                chain(nc.vector.tensor_copy(farT[:], mm[0:1, 1, 128:129]))
                nc.vector.tensor_scalar(flag[:], farT[:], 0.0, None, ALU.is_gt)
                dve.wait_ge(s_x, 32)
                layer_norm(dve, chain, s_sq, s_sqd)
                chain(nc.vector.tensor_scalar(work[:], work[:], 0.0, None, ALU.max))
                dve.wait_ge(s_deg, NG)
                nc.vector.tensor_scalar(dis[:], mm[:, 0, 0:NB], 1.0, None, ALU.add).then_inc(s_sq, 1)
                dve.wait_ge(s_sqd, 2)
                chain(nc.vector.reciprocal(dis[:], dis[:]))
                chain(nc.vector.tensor_tensor(tab[:], work[:], bcast(dis[:], D), ALU.mult))
                for c in range(NC + 2):
                    if c < NC:
                        dve.sem_inc(q0["rows"], 1)
                    split_dve(dve, q0, c)

            @block.tensor
            def _(pe):
                pe.wait_ge(s_const, 1)
                nc.tensor.matmul(mm[:, 0, 0:NB], lhsT=zeros_b[:, 0:P], rhs=zeros_b[:, 0:NB], start=True, stop=True)
                with pe.Fori(0, NG // 2) as it:
                    for b in range(2):
                        pe.wait_ge(s_hot, it * 2 + (b + 1))
                        for t in range(TPG):
                            for h in range(2):
                                last = nc.tensor.matmul(mm[h * HALF:(h + 1) * HALF, 0, 0:NB], lhsT=hot_lo[:, b, t, :],
                                                        rhs=hot_hi[:, b, t, h:2 * NB:2],
                                                        start=False, stop=True, skip_group_check=True)
                        last.then_inc(s_deg, 1)
                pe.wait_ge(s_gm, 1)
                nc.tensor.transpose(tp[0:NG, 0, 0:P], gmin[:], ident[:]).then_inc(s_gt, 1)
                pe.wait_ge(s_bd, 1)
                nc.tensor.matmul(mm[:, 1, 0:2 * NG], lhsT=ones[0:NG, :], rhs=bdiag[:], start=True, stop=True).then_inc(s_bb, 1)
                pe.wait_ge(s_far, 1)
                nc.tensor.matmul(mm[0:1, 1, 128:129], lhsT=far[:], rhs=ones[:, 0:1], start=True, stop=True).then_inc(s_ft, 1)
                zero_sums()

        def turn_chunk(q, c, source, wide):
            k0, n = chunk(c)
            for i in range(n):
                last = nc.tensor.transpose(tp[0:(2 * D if wide else D), c % 2, i * P:(i + 1) * P],
                                           source[:, k0 + i, :], ident[:])
            last.then_inc(q["turned"], 1)

        def copy_chunk(q, c, wide):
            k0, n = chunk(c)
            h = 2 * D if wide else D
            nc.scalar.copy(catT[0:h, k0 * P:(k0 + n) * P], tp[0:h, c % 2, 0:n * P]).then_inc(q["copied"], 1)

        def product_chunk(q, c, weights, rows_):
            k0, n = chunk(c)
            for i in range(n):
                last = nc.tensor.matmul(mm[:, c % 2, i * D:(i + 1) * D], lhsT=catT[0:rows_, (k0 + i) * P:(k0 + i + 1) * P],
                                        rhs=weights, start=True, stop=True)
            last.then_inc(q["done"], 1)

        def product(c):
            n = chunk(c)[1]
            return mm[:, c % 2, 0:n * D].rearrange("p (k d) -> p k d", d=D)

        def over(bias, n):
            return bias.unsqueeze(1).to_broadcast([P, n, D])

        def pe_sweep(pe, q, source, weights, wide, before=None):
            for c in range(NC + 1):
                if c < NC:
                    pe.wait_ge(q["ready"], c + 1)
                    if c >= 2:
                        pe.wait_ge(q["copied"], c - 1)
                    elif before is not None:
                        pe.wait_ge(before["copied"], NC)
                    turn_chunk(q, c, source, wide)
                if c >= 1:
                    pe.wait_ge(q["copied"], c)
                    if c >= 3:
                        pe.wait_ge(q["final"], c - 2)
                    elif before is not None:
                        pe.wait_ge(before["final"], NC)
                    product_chunk(q, c - 1, weights, 2 * D if wide else D)

        def act_sweep(act, q, wide):
            for c in range(NC):
                act.wait_ge(q["turned"], c + 1)
                copy_chunk(q, c, wide)

        def first_windows():
            nc.vector.tensor_copy(rel[:], rel0[:])
            nc.vector.tensor_copy(col[:], col0[:])

        convolve(tables[0], 0)
        q = node_sems("gcn1")
        with nc.Block() as block:
            @block.sync
            def _(sp):
                clear_edge_sems(sp)
                store_table(sp, q, tables[1])

            @block.gpsimd
            def _(pool):
                clear_gather_sems(pool)

            @block.vector
            def _(dve):
                chain = Chain(dve, q["dve"])
                for c in range(NC):
                    k0, n = chunk(c)
                    w = work[:, k0:k0 + n, :]
                    chain(nc.vector.tensor_tensor(w, agg_chunk(c), tab[:, k0:k0 + n, :], ALU.add))
                    nc.vector.tensor_tensor(w, w, bcast(dis[:, k0:k0 + n], D), ALU.mult).then_inc(q["ready"], 1)
                for c in range(NC + 2):
                    if c < NC:
                        k0, n = chunk(c)
                        dve.wait_ge(q["done"], c + 1)
                        nc.vector.tensor_tensor(tab[:, k0:k0 + n, :], agg[:, c % 4 * 512:c % 4 * 512 + n * D].rearrange(
                            "p (k d) -> p k d", d=D), bcast(dis[:, k0:k0 + n], D), ALU.mult).then_inc(q["rows"], 1)
                    split_dve(dve, q, c)
                first_windows()

            @block.scalar
            def _(act):
                for c in range(NC + 3):
                    if c < NC:
                        act.wait_ge(q["turned"], c + 1)
                        copy_chunk(q, c, False)
                    if 1 <= c <= NC:
                        k0, n = chunk(c - 1)
                        act.wait_ge(q["mid"], c)
                        nc.scalar.activation(midT[:, k0 * P:(k0 + n) * P], mm[:, (c - 1) % 2, 0:n * P], ACT.Relu,
                                             bias=b1_s[:]).then_inc(q["relu"], 1)
                    if c >= 2:
                        split_act(act, q, c - 2)

            @block.tensor
            def _(pe):
                for c in range(NC + 2):
                    if c < NC:
                        pe.wait_ge(q["ready"], c + 1)
                        if c >= 2:
                            pe.wait_ge(q["copied"], c - 1)
                        turn_chunk(q, c, work, False)
                    if 1 <= c <= NC:
                        k0, n = chunk(c - 1)
                        pe.wait_ge(q["copied"], c)
                        if c >= 3:
                            pe.wait_ge(q["relu"], c - 2)
                        nc.tensor.matmul(mm[:, (c - 1) % 2, 0:n * P], lhsT=W1_s[:], rhs=catT[0:D, k0 * P:(k0 + n) * P],
                                         start=True, stop=True).then_inc(q["mid"], 1)
                    if c >= 2:
                        k0, n = chunk(c - 2)
                        pe.wait_ge(q["relu"], c - 1)
                        pe.wait_ge(q["ready"], min(NC, 2 * (c - 1)))
                        if c >= 6:
                            pe.wait_ge(q["rows"], c - 5)
                        for i in range(n):
                            k = k0 + i
                            at = (c - 2) % 4 * 512 + i * D
                            last = nc.tensor.matmul(agg[:, at:at + D], lhsT=midT[:, k * P:(k + 1) * P],
                                                    rhs=W2_s[:], start=True, stop=True, skip_group_check=True)
                        last.then_inc(q["done"], 1)
                pe.wait_ge(q["final"], NC)
                zero_sums()

        convolve(tables[1], 1)
        q2 = node_sems("gcn2")
        s_sq2, s_sqd2 = sem("s_sq2"), sem("s_sqd2")
        with nc.Block() as block:
            @block.sync
            def _(sp):
                clear_edge_sems(sp)
                store_table(sp, q2, tables[2])

            @block.gpsimd
            def _(pool):
                clear_gather_sems(pool)

            @block.vector
            def _(dve):
                chain = Chain(dve, q2["dve"])
                sums = agg[:, 0:NB * D].rearrange("p (k d) -> p k d", d=D)
                chain(nc.vector.tensor_tensor(work[:], sums, tab[:], ALU.add))
                chain(nc.vector.tensor_tensor(work[:], work[:], bcast(dis[:], D), ALU.mult))
                chain(nc.vector.tensor_tensor(work[:], work[:], over(b2_s[:], NB), ALU.add))
                chain(nc.vector.tensor_tensor(xs[:], xs[:], work[:], ALU.add))
                layer_norm(dve, chain, s_sq2, s_sqd2)
                for c in range(NC):
                    k0, n = chunk(c)
                    nc.vector.tensor_scalar(cat[:, k0:k0 + n, 0:D], work[:, k0:k0 + n, :], 0.0, None,
                                            ALU.max).then_inc(q2["ready"], 1)
                for c in range(NC):
                    k0, n = chunk(c)
                    dve.wait_ge(q2["done"], c + 1)
                    nc.vector.tensor_tensor(tab[:, k0:k0 + n, :], product(c), over(bmsg_s[:, 0, :], n),
                                            ALU.add).then_inc(q2["final"], 1)
                first_windows()

            @block.scalar
            def _(act):
                act.wait_ge(s_sq2, 1)
                nc.scalar.activation(stat[:, 2, :], stat[:, 2, :], ACT.Sqrt).then_inc(s_sqd2, 1)
                act_sweep(act, q2, False)

            @block.tensor
            def _(pe):
                pe.wait_ge(q2["ready"], NC)
                zero_sums()
                pe_sweep(pe, q2, cat[:, :, 0:D], top_s[:, 0, :], False)

        def gather_sums(q):
            for c in range(NC):
                k0, n = chunk(c)
                nc.vector.tensor_copy(cat[:, k0:k0 + n, D:2 * D], agg_chunk(c)).then_inc(q["ready"], 1)

        def apply_chunk(dve, chain, q, layer, c, to):
            k0, n = chunk(c)
            dve.wait_ge(q["done"], c + 1)
            w = work[:, k0:k0 + n, :]
            chain(nc.vector.tensor_tensor(w, product(c), over(bapp_s[:, layer, :], n), ALU.add))
            return nc.vector.scalar_tensor_tensor(to, w, 0.0, cat[:, k0:k0 + n, 0:D], ALU.max, ALU.add)

        sum_over_edges(tables[2], 0)
        q3, q4 = node_sems("app1"), node_sems("msg2")
        with nc.Block() as block:
            @block.sync
            def _(sp):
                clear_edge_sems(sp)
                store_table(sp, q4, tables[3])

            @block.gpsimd
            def _(pool):
                clear_gather_sems(pool)

            @block.vector
            def _(dve):
                chain = Chain(dve, q3["dve"])
                gather_sums(q3)
                for c in range(NC):
                    k0, n = chunk(c)
                    apply_chunk(dve, chain, q3, 0, c, cat[:, k0:k0 + n, 0:D]).then_inc(q3["final"], 1)
                for c in range(NC):
                    k0, n = chunk(c)
                    dve.wait_ge(q4["done"], c + 1)
                    nc.vector.tensor_tensor(tab[:, k0:k0 + n, :], product(c), over(bmsg_s[:, 1, :], n),
                                            ALU.add).then_inc(q4["final"], 1)
                first_windows()

            @block.scalar
            def _(act):
                act_sweep(act, q3, True)
                act_sweep(act, q4, False)

            @block.tensor
            def _(pe):
                pe.wait_ge(q3["ready"], NC)
                zero_sums()
                pe_sweep(pe, q3, cat, app_s[:, 0, :], True)
                pe_sweep(pe, dict(q4, ready=q3["final"]), cat[:, :, 0:D], top_s[:, 1, :], False, before=q3)

        sum_over_edges(tables[3], 1)
        q5 = node_sems("app2")
        with nc.Block() as block:
            @block.sync
            def _(sp):
                for c in range(NC):
                    k0, n = chunk(c)
                    sp.wait_ge(q5["final"], c + 1)
                    if c < NC - 1:
                        sp.dma_start(out[k0 * P:(k0 + n) * P, :].rearrange("(k p) d -> p k d", p=P),
                                     work[:, k0:k0 + n, :]).then_inc(q5["out"], 16)
                    else:
                        sp.dma_start(out[k0 * P:N, :], work[0:NTAIL, k0, :]).then_inc(q5["out"], 16)
                sp.wait_ge(q5["out"], 16 * NC)

            @block.vector
            def _(dve):
                chain = Chain(dve, q5["dve"])
                gather_sums(q5)
                for c in range(NC):
                    k0, n = chunk(c)
                    w = work[:, k0:k0 + n, :]
                    chain(apply_chunk(dve, chain, q5, 1, c, w))
                    nc.vector.tensor_tensor(w, w, xs[:, k0:k0 + n, :], ALU.add).then_inc(q5["final"], 1)

            @block.scalar
            def _(act):
                act_sweep(act, q5, True)

            @block.tensor
            def _(pe):
                pe_sweep(pe, q5, cat, app_s[:, 1, :], True)


_INS = ['x', 'src', 'dst', 'edge_attr_64', 'L0_gnn_W1', 'L0_gnn_b1', 'L0_gnn_W2', 'L0_gnn_b2',
        'L1_gnn_W1_msg', 'L1_gnn_b1_msg', 'L1_gnn_W1_app', 'L1_gnn_b1_app',
        'L1_gnn_W2_msg', 'L1_gnn_b2_msg', 'L1_gnn_W2_app', 'L1_gnn_b2_app']
_OUT = (3125, 64)


def kernel(**inputs):
    import numpy as _np
    import concourse.bacc as _bacc
    from concourse import mybir as _mybir
    from concourse.bass_utils import run_bass_kernel_spmd as _run

    nc = _bacc.Bacc("TRN2", target_bir_lowering=False, num_devices=1)
    arrays, args = {}, []
    for name in _INS:
        a = _np.ascontiguousarray(inputs[name])
        arrays[f"in_{name}_dram"] = a
        args.append(nc.dram_tensor(f"in_{name}_dram", a.shape, _mybir.dt.from_np(a.dtype), kind="ExternalInput").ap())
    args.append(nc.dram_tensor("out_0_dram", _OUT, _mybir.dt.float32, kind="ExternalOutput").ap())
    gnn_kernel(nc, *args)
    r = _run(nc, [arrays], core_ids=[0])
    return r.results[0]["out_0_dram"]
```

```python
import concourse.bass as bass
from concourse import mybir
from contextlib import ExitStack

P = 128
N = 3125
E = 53125
D = 64
MID = 128
NB = -(-N // P)
NTAIL = N - (NB - 1) * P
AGGB = NB + 1
TPG = 8
GE = P * TPG
NG = -(-E // GE)
ETAIL = E - (NG - 1) * GE
TFULL = ETAIL // TPG
TREST = ETAIL - TFULL * TPG
R = 4
NIT = NG // R
WIN = 2 * P
SHIFTS = -(-NB // 2) - 1
HALF = P // 2
DG = 4
NO_NODE = 1 << 20
GATHERED = 12
SW = 12
UT = 10
DW = UT * SW
T0 = GATHERED * TPG
NU = (NG * TPG - T0) // UT
TPP = 4
TP = NG * TPG // TPP
TE = TPP * P
assert NG % R == 0 and NG % DG == 0 and NG // DG % 2 == 1
assert E > (NG * TPG - 1) * P
assert TP <= P and DW <= P and NB * SW <= 512 and NB * SW % 2 == 0 and T0 + NU * UT == NG * TPG
EARLY = 8
CTURNS = GATHERED // R
IN_TURN = (NU - EARLY) // CTURNS
BEHIND = IN_TURN // R
KSLOTS = 4
BY_PE = (1, 2, 1, 2)
PE_TILES = max(BY_PE)
FAR = 2048.0
WARM_UP = 6
CB = 4
NC = -(-NB // CB)
EPS = 1e-5

fp32 = mybir.dt.float32
bf16 = mybir.dt.bfloat16
fp16 = mybir.dt.float16
i32 = mybir.dt.int32
ALU = mybir.AluOpType
ACT = mybir.ActivationFunctionType
AX = mybir.AxisListType


def chunk(c):
    return c * CB, min(CB, NB - c * CB)


class Chain:

    def __init__(self, engine, sem):
        self.engine, self.sem, self.n = engine, sem, 0

    def __call__(self, ins):
        self.n += 1
        ins.then_inc(self.sem, 1)
        self.engine.wait_ge(self.sem, self.n)


def gnn_kernel(nc, x, src, dst, efeat, W1, b1, W2, b2,
               W1_msg, b1_msg, W1_app, b1_app, W2_msg, b2_msg, W2_app, b2_app, out):
    ctx = ExitStack()
    with ctx:
        def sb(name, shape, dt=fp32):
            return ctx.enter_context(nc.sbuf_tensor(name, shape, dt))

        def sem(name):
            return ctx.enter_context(nc.semaphore(name))

        tables = [nc.dram_tensor(f"table{i}", (P * NB, 3 * D if i < 2 else D), bf16 if i < 2 else fp32).ap()
                  for i in range(4)]
        kept = nc.dram_tensor("kept", (NU, P, NB * DW), fp16).ap()

        src_i = sb("src_i", [P, NG, TPG], i32)
        dst_i = sb("dst_i", [P, NG, TPG], i32)
        tmp_i = sb("tmp_i", [P, NG, TPG], i32)
        row_i = sb("row_i", [P, NG + R, TPG], i32)
        dst_f = sb("dst_f", [P, NG, TPG])
        rel0 = sb("rel0", [P, NG, TPG])
        rel = sb("rel", [P, NG, TPG])
        rel2 = sb("rel2", [P, NG, TPG, 2], bf16)
        src_lo2 = sb("src_lo2", [P, NG, TPG, 2], fp16)
        pair2 = sb("pair2", [P, NG, TPG, 2], fp16)
        dst_lo2 = sb("dst_lo2", [P, NG, TPG, 2], fp16)
        dst_hi2 = sb("dst_hi2", [P, NG, TPG, 2], fp16)
        outside = sb("outside", [P, NG, TPG])
        src_t = sb("src_t", [TP, TE], i32)
        dst_t = sb("dst_t", [TP, TE], i32)
        lo_t = sb("lo_t", [TP, TE])
        pair_t = sb("pair_t", [TP, TE])
        tmp_t = sb("tmp_t", [TP, TE])
        first_t = sb("first_t", [TP, TPP])
        far_t = sb("far_t", [TP, 1])
        behind_i = sb("behind_i", [TP, TPP, NU], i32)
        behind = sb("behind", [TP, TPP, NU])
        member = sb("member", [TP, TPP, NU])
        opens = sb("opens", [TP, TPP, NU])
        number = sb("number", [TP, TPP])
        block_i = sb("block_i", [TP, TPP], i32)
        block_t = sb("block_t", [TP, TPP])
        tile_i = sb("tile_i", [TP, DW], i32)
        tile_f = sb("tile_f", [TP, DW])
        of_tile = sb("of_tile", [TP, TPP, DW])
        of_unit = sb("of_unit", [TP, TPP, NU])
        gmin = sb("gmin", [P, NG])
        bmin = sb("bmin", [NG, 2])
        bmin_i = sb("bmin_i", [NG, 1], i32)
        bdiag = sb("bdiag", [NG, NG])
        base = sb("base", [P, NG])
        offset = sb("offset", [DW, NU])
        target = sb("target", [DW, NU])
        target_far = sb("target_far", [DW, NU])
        far_u = sb("far_u", [DW, 1])
        unit_col = sb("unit_col", [1, NU], i32)
        col0 = sb("col0", [1, NG], i32)
        col = sb("col", [1, NG], i32)
        far = sb("far", [P, 1])
        farT = sb("farT", [1, 1])
        flag = sb("flag", [1, 1], i32)
        idx = sb("idx", [P, R, TPG], i32)
        rows_mem = sb("rows_mem", [P, R * TPG * 3 * D // 2])
        rows3 = rows_mem[:, :].bitcast(bf16).rearrange("p (r n) -> p r n", r=R)
        rows = rows_mem[:, 0:R * TPG * D].rearrange("p (r n) -> p r n", r=R)
        edge_mem = sb("edge_mem", [P, NB * 2 * D + R * TPG * D + 8 * P + 5 * TPG * D])
        at = NB * 2 * D
        cat = edge_mem[:, 0:at].rearrange("p (k d) -> p k d", k=NB)
        ef = edge_mem[:, at:at + R * TPG * D].rearrange("p (r n) -> p r n", r=R)
        at += R * TPG * D
        efT = edge_mem[:, at:at + 8 * P].rearrange("p (r n) -> p r n", r=2)
        at += 8 * P
        msg = edge_mem[:, at:at + 2 * TPG * D].rearrange("p (r n) -> p r n", r=2)
        at += 2 * TPG * D
        msg3 = edge_mem[:, at:at + 3 * TPG * D].bitcast(bf16).rearrange("p (r a n) -> p r a n", r=2, a=3)
        counts = sb("counts", [P, KSLOTS, NB * DW], fp16)
        parts = sb("parts", [P, NB, 3, D], bf16)
        dsum = sb("dsum", [DW, 2, D])
        place = sb("place", [DW, 2, WIN])
        diag_i = sb("diag_i", [P, WIN], i32)
        diag_f = sb("diag_f", [P, WIN])
        pe_lo = sb("pe_lo", [P, NG, PE_TILES], bf16)
        pe_hi = sb("pe_hi", [P, NG, PE_TILES], bf16)
        chosen = sb("chosen", [P, PE_TILES, P], bf16)
        block2 = sb("block2", [P, NB, 2], bf16)
        ident_b = sb("ident_b", [P, P], bf16)
        onehot = sb("onehot", [P, 2, TPG, WIN], bf16)
        iota_i = sb("iota_i", [P, NB * SW], i32)
        iota_f = sb("iota_f", [P, P])
        iota_b = sb("iota_b", [P, WIN], bf16)
        iota_h = sb("iota_h", [P, NB * SW], fp16)
        part_i = sb("part_i", [P, 1], i32)
        part_f = sb("part_f", [P, 1])
        ident = sb("ident", [P, P])
        zeros_b = sb("zeros_b", [P, 512], bf16)
        ones = sb("ones", [P, P])
        pool_mem = sb("pool_mem", [P, 2 * NB * P])
        catT = pool_mem[:, 0:NB * P]
        midT = pool_mem[:, NB * P:2 * NB * P]
        hot16 = pool_mem[:, :].bitcast(fp16)
        hot_node = pool_mem[:, 0:NB * P].bitcast(bf16).rearrange("p (b k n) -> p b k n", b=2, k=NB)
        at = 2 * DG * TPG * HALF
        hot_lo = hot16[:, 0:at].rearrange("p (b t n) -> p b t n", b=2, t=DG * TPG)
        hot_hi = hot16[:, at:at + 2 * DG * TPG * 2 * NB].rearrange("p (b t n) -> p b t n", b=2, t=DG * TPG)
        at = 2 * UT * NB * SW
        hot_pair = hot16[:, 0:at].rearrange("p (b t n) -> p b t n", b=2, t=UT)
        hot_src = hot16[:, at:at + 2 * UT * P].rearrange("p (b t n) -> p b t n", b=2, t=UT)
        lower = sb("lower", [HALF, 2 * NB])
        up = sb("up", [HALF, P])
        dis = sb("dis", [P, NB])
        scale = sb("scale", [P, NB])
        xs = sb("xs", [P, NB, D])
        tab = sb("tab", [P, NB, D])
        work = sb("work", [P, NB, D])
        stat = sb("stat", [P, 4, NB])
        W1_s = sb("W1_s", [D, MID])
        W2_s = sb("W2_s", [MID, D])
        b1_s = sb("b1_s", [MID, 1])
        b2_s = sb("b2_s", [P, D])
        top_s = sb("top_s", [D, 2, D])
        bot_s = sb("bot_s", [P, 2, P])
        app_s = sb("app_s", [P, 2, D])
        bmsg_s = sb("bmsg_s", [P, 2, D])
        bapp_s = sb("bapp_s", [P, 2, D])

        agg = ctx.enter_context(nc.psum_tensor("agg", [P, 2048], fp32))
        tp = ctx.enter_context(nc.psum_tensor("tp", [P, 2, 512], fp32))
        mm = ctx.enter_context(nc.psum_tensor("mm", [P, 2, 512], fp32))

        def agg_chunk(c):
            k, n = chunk(c)
            return agg[:, k * D:(k + n) * D].rearrange("p (k d) -> p k d", d=D)

        staged = sem("staged")
        started = sem("started")
        gathered = [sem(f"gathered{j}") for j in range(R)]
        loaded = [sem(f"loaded{j}") for j in range(R)]
        hot_ready = sem("hot_ready")
        summed = sem("summed")
        turned = sem("turned")
        copied = sem("copied")
        projected = sem("projected")
        added = sem("added")
        term1 = sem("term1")
        rest = sem("rest")
        term2 = sem("term2")
        msg_ready = sem("msg_ready")
        spread = sem("spread")
        matched = sem("matched")
        picked = sem("picked")
        node_ready = sem("node_ready")
        fetched = sem("fetched")
        edge_sems = [staged, started, *loaded, hot_ready, summed, turned, copied, projected, added, term1, rest,
                     term2, msg_ready, spread, matched, picked, node_ready, fetched]
        pair_ready = sem("pair_ready")
        bank_full = sem("bank_full")
        bank_copied = sem("bank_copied")
        stored = [sem(f"stored{u}") for u in range(2)]
        reloaded = [sem(f"reloaded{u}") for u in range(KSLOTS)]
        applied = sem("applied")
        reduced = sem("reduced")
        placed = sem("placed")
        edge_sems += [pair_ready, bank_full, bank_copied, *stored, *reloaded, applied, reduced, placed]

        def one_hots(out, columns, numbers, tile):
            tiles, n = out.shape[1], out.shape[2] // 2
            return nc.vector.tensor_tensor(
                out.rearrange("p t (n x) -> p t n x", x=2),
                columns[:, 0:2 * n].rearrange("p (n x) -> p n x", x=2).unsqueeze(1).to_broadcast([P, tiles, n, 2]),
                numbers[:, :, :, :].rearrange("p g t x -> p (g t) x")[:, bass.ds(tile, tiles), :].unsqueeze(2)
                .to_broadcast([P, tiles, n, 2]), ALU.is_equal)

        def columns(of, g, n):
            return nc.values_load_multi_w_load_instructions(
                of[0:1, bass.ds(g, n)], engines=(mybir.EngineType.PE,), min_val=0, max_val=(NB - 1) * D,
                skip_runtime_bounds_check_because="DVE has clamped them to the sums' columns")[1]

        def twice(to, of):
            for x in range(2):
                last = nc.vector.tensor_copy(to[:, :, :, x], of)
            return last

        def stage(g, j):
            nc.vector.tensor_copy(idx[:, j:j + 1, :], row_i[:, bass.ds(g, 1), :]).then_inc(staged, 1)

        def window_hots(g, j):
            one_hots(onehot[:, j % 2, :, :], iota_b, rel2, g * TPG).then_inc(hot_ready, 1)

        def add_rows(j, at, term):
            for w in range(2):
                sums = agg[:, bass.ds(at + w * D, D)]
                for t in range(TPG):
                    for a in range(3):
                        last = nc.tensor.matmul(sums, lhsT=onehot[:, j % 2, t, w * P:(w + 1) * P], rhs=term(t, a),
                                                start=False, stop=True, skip_group_check=True)
            last.then_inc(summed, 1)

        def gather_pass(table, groups):
            with nc.gpsimd.Fori(0, groups // R) as it:
                for j in range(R):
                    nc.gpsimd.wait_ge(staged, it * R + (j + 1))
                    nc.gpsimd.sem_inc(started, 1)
                    for t in range(TPG):
                        nc.gpsimd.indirect_dma_start(
                            out=rows3[:, j, 3 * t * D:3 * (t + 1) * D], out_offset=None, in_=table[:, :],
                            in_offset=bass.IndirectOffsetOnAxis(ap=idx[:, j, t:t + 1], axis=0),
                        ).then_inc(gathered[j], 16)
            for j in range(R):
                nc.gpsimd.wait_ge(gathered[j], groups // R * TPG * 16)

        def scatter_rows(pe, g, j, at):
            pe.wait_ge(hot_ready, g + 1)
            pe.wait_ge(gathered[j], (g - j) * (TPG * 16 // R) + TPG * 16)
            add_rows(j, at, lambda t, a: rows3[:, j, (3 * t + a) * D:(3 * t + a + 1) * D])

        def edge_pass(table):
            with nc.Block() as block:
                @block.gpsimd
                def _(pool):
                    gather_pass(table, NG)

                @block.vector
                def _(dve):
                    def step(g, j, first):
                        if not (first and j < 2):
                            dve.wait_ge(summed, g - 1)
                        window_hots(g, j)
                        if not (first and j == 0):
                            dve.wait_ge(summed, g)
                            stage(g + (R - 1), (j - 1) % R)

                    for j in range(R):
                        stage(j, j)
                    for j in range(R):
                        step(j, j, True)
                    with dve.Fori(1, NIT) as it:
                        for j in range(R):
                            step(it * R + j, j, False)

                @block.tensor
                def _(pe):
                    with pe.Fori(0, NIT) as it:
                        at = columns(col, it * R, R)
                        for j in range(R):
                            scatter_rows(pe, it * R + j, j, at[j])

        def message_pass(table, layer):
            per_turn = sum(BY_PE)
            assert per_turn % 2 == 0 and R % 2 == 0

            def by_pool(j):
                return TPG - BY_PE[j]

            def pe_tiles(it, j):
                base = j // R * per_turn + sum(BY_PE[:j % R])
                return [(it * R + j, by_pool(j % R) + u, it * per_turn + (base + u), (base + u) % 2)
                        for u in range(BY_PE[j % R])]

            with nc.Block() as block:
                @block.gpsimd
                def _(pool):
                    with pool.Fori(0, NIT) as it:
                        for j in range(R):
                            pool.wait_ge(staged, it * R + (j + 1))
                            pool.sem_inc(started, 1)
                            for t in range(by_pool(j)):
                                nc.gpsimd.indirect_dma_start(
                                    out=rows[:, j, t * D:(t + 1) * D], out_offset=None, in_=table[:, :],
                                    in_offset=bass.IndirectOffsetOnAxis(ap=idx[:, j, t:t + 1], axis=0),
                                ).then_inc(gathered[j], 16)
                    for j in range(R):
                        pool.wait_ge(gathered[j], NIT * by_pool(j) * 16)

                @block.sync
                def _(sp):
                    def load(g, j):
                        sp.dma_start(ef[:, j, :], efeat[bass.ds(g * GE, GE), :].rearrange(
                            "(p t) f -> p (t f)", t=TPG)).then_inc(loaded[j], 16)

                    for j in range(R):
                        load(j, j)
                    with sp.Fori(1, NIT - 1) as it:
                        for j in range(R):
                            sp.wait_ge(turned, (it - 1) * R + (j + 1))
                            load(it * R + j, j)
                    for j in range(R):
                        sp.wait_ge(turned, (NIT - 2) * R + j + 1)
                        if j < R - 1:
                            load((NIT - 1) * R + j, j)
                    e0 = (NG - 1) * GE
                    sp.dma_start(ef[0:TFULL, R - 1, :], efeat[e0:e0 + TFULL * TPG, :].rearrange(
                        "(p t) f -> p (t f)", t=TPG)).then_inc(loaded[R - 1], 16)
                    sp.dma_start(ef[TFULL:TFULL + 1, R - 1, 0:TREST * D], efeat[E - TREST:E, :].rearrange(
                        "(p t) f -> p (t f)", t=TREST)).then_inc(loaded[R - 1], 16)

                @block.vector
                def _(dve):
                    def pick(g, tiles):
                        n = tiles[0][2]
                        dve.wait_ge(spread, g + 1)
                        if not isinstance(n, int) or n > 0:
                            dve.wait_ge(node_ready, n)
                        to = chosen[:, 0:len(tiles), :]
                        sources = tp[:, 1, 0:len(tiles) * 2 * P].rearrange("p (u x n) -> p u x n", u=len(tiles), x=2)
                        nc.vector.tensor_scalar(to, sources[:, :, 0, :], part_f[:], None, ALU.is_equal
                                                ).then_inc(matched, 1)
                        dve.wait_ge(matched, g + 1)
                        nc.vector.tensor_tensor(to, sources[:, :, 1, :], to, ALU.mult).then_inc(picked, 1)

                    def node_hots(g, u, n, b):
                        dve.wait_ge(picked, g + 1)
                        if not isinstance(n, int) or n >= 2:
                            dve.wait_ge(fetched, n - 1)
                        nc.vector.tensor_tensor(
                            hot_node[:, b, :, :].rearrange("p k (n x) -> p k n x", x=2),
                            chosen[:, u, :].rearrange("p (n x) -> p n x", x=2).unsqueeze(1).to_broadcast([P, NB, P // 2, 2]),
                            block2[:, :, :].unsqueeze(2).to_broadcast([P, NB, P // 2, 2]), ALU.is_equal
                        ).then_inc(node_ready, 1)

                    def step(it, j, first, last):
                        g = it * R + j
                        ahead = [] if last and j >= R - 2 else pe_tiles(it, j + 2)
                        dve.wait_ge(projected, g + 1)
                        dve.wait_ge(gathered[j], (g - j) * (by_pool(j) * 16 // R) + by_pool(j) * 16)
                        nc.vector.tensor_tensor(msg[:, j % 2, :], mm[:, j % 2, :], rows[:, j, :],
                                                ALU.add).then_inc(added, 1)
                        dve.wait_ge(added, g + 1)
                        stage(g + R, j)
                        if not (last and j == R - 1):
                            if not (first and j == 0):
                                dve.wait_ge(summed, g)
                            window_hots(g + 1, j + 1)
                        dve.wait_ge(term1, g + 1)
                        nc.vector.scalar_tensor_tensor(msg[:, j % 2, :], msg[:, j % 2, :], 0.0,
                                                       msg3[:, j % 2, 0, :], ALU.max, ALU.subtract).then_inc(rest, 1)
                        if ahead:
                            pick(g + 2, ahead)
                        dve.wait_ge(term2, g + 1)
                        nc.vector.tensor_tensor(msg3[:, j % 2, 2, :], msg[:, j % 2, :], msg3[:, j % 2, 1, :],
                                                ALU.subtract).then_inc(msg_ready, 1)
                        for u, (_, _, n, b) in enumerate(ahead):
                            node_hots(g + 2, u, n, b)

                    for j in range(R):
                        stage(j, j)
                    window_hots(0, 0)
                    for j in range(2):
                        pick(j, pe_tiles(0, j))
                        for u, (_, _, n, b) in enumerate(pe_tiles(0, j)):
                            node_hots(j, u, n, b)
                    for j in range(R):
                        step(0, j, True, False)
                    with dve.Fori(1, NIT - 1) as it:
                        for j in range(R):
                            step(it, j, False, False)
                    for j in range(R):
                        step(NIT - 1, j, False, True)

                @block.scalar
                def _(act):
                    def copy(g, b):
                        act.wait_ge(turned, g + 1)
                        nc.scalar.copy(efT[:, b, :], tp[:, 0, :]).then_inc(copied, 1)

                    def relu(g, b):
                        act.wait_ge(added, g + 1)
                        nc.scalar.activation(msg3[:, b, 0, :], msg[:, b, :], ACT.Relu).then_inc(term1, 1)
                        act.wait_ge(rest, g + 1)
                        nc.scalar.copy(msg3[:, b, 1, :], msg[:, b, :]).then_inc(term2, 1)

                    copy(0, 0)
                    copy(1, 1)
                    with act.Fori(0, NIT - 1) as it:
                        for j in range(R):
                            relu(it * R + j, j % 2)
                            copy(it * R + (j + 2), j % 2)
                    for j in range(R):
                        g = (NIT - 1) * R + j
                        relu(g, j % 2)
                        if g + 2 < NG:
                            copy(g + 2, j % 2)

                @block.tensor
                def _(pe):
                    def turn(g, j, count):
                        pe.wait_ge(loaded[j], count)
                        for q in range(TPG // 2):
                            last = nc.tensor.transpose(tp[:, 0, q * P:(q + 1) * P],
                                                       ef[:, j, q * P:(q + 1) * P], ident[:])
                        last.then_inc(turned, 1)

                    def spread_sources(g, tiles):
                        if not isinstance(g, int) or g > 0:
                            pe.wait_ge(picked, g)
                        for u, (_, tile, _, _) in enumerate(tiles):
                            for i, of in enumerate((pe_lo, pe_hi)):
                                t = tile - (TPG - PE_TILES)
                                last = nc.tensor.matmul(
                                    tp[:, 1, (2 * u + i) * P:(2 * u + i + 1) * P], rhs=ident_b[:], start=True, stop=True,
                                    lhsT=of[:, bass.ds(g, 1), t:t + 1].rearrange("p a b -> p (a b)").to_broadcast([P, P]))
                        last.then_inc(spread, 1)

                    def project(it, j, more):
                        g = it * R + j
                        pe.wait_ge(copied, g + 1)
                        for q in range(TPG // 2):
                            last = nc.tensor.matmul(mm[:, j % 2, q * P:(q + 1) * P],
                                                    lhsT=efT[:, j % 2, q * P:(q + 1) * P], rhs=bot_s[:, layer, :],
                                                    start=True, stop=True)
                        for u, (_, tile, n, b) in enumerate(pe_tiles(it, j)):
                            pe.wait_ge(node_ready, n + 1)
                            if u == 0 and more:
                                spread_sources(g + 1, pe_tiles(it, j + 1))
                            for k in range(NB):
                                for a in range(3):
                                    last = nc.tensor.matmul(mm[:, j % 2, tile * D:(tile + 1) * D],
                                                            lhsT=hot_node[:, b, k, :], rhs=parts[:, k, a, :],
                                                            start=False, stop=True, skip_group_check=True)
                            last.then_inc(fetched, 1)
                        pe.wait_ge(fetched, n + 1)
                        pe.sem_inc(projected, 1)

                    def scatter(g, j, at):
                        pe.wait_ge(hot_ready, g + 1)
                        pe.wait_ge(msg_ready, g + 1)
                        add_rows(j, at, lambda t, a: msg3[:, j % 2, a, t * D:(t + 1) * D])

                    spread_sources(0, pe_tiles(0, 0))
                    for j in range(2):
                        turn(j, j, 16)
                        project(0, j, True)
                    with pe.Fori(0, NIT - 1) as it:
                        at = columns(col, it * R, R)
                        for j in range(R):
                            turn(it * R + (j + 2), (j + 2) % R, it * 16 + (16 if j < R - 2 else 32))
                            scatter(it * R + j, j, at[j])
                            project(it, j + 2, True)
                    at = columns(col, (NIT - 1) * R, R)
                    for j in range(R):
                        g = (NIT - 1) * R + j
                        if g + 2 < NG:
                            turn(g + 2, j + 2, NIT * 16 + (16 if g + 2 == NG - 1 else 0))
                        scatter(g, j, at[j])
                        if g + 2 < NG:
                            project(NIT - 1, j + 2, g + 3 < NG)

        def convolution_pass(table, which):
            making = which == 0
            assert GATHERED % R == 0 and EARLY + BEHIND * R * CTURNS == NU and EARLY % KSLOTS == IN_TURN % KSLOTS == 0

            with nc.Block() as block:
                @block.gpsimd
                def _(pool):
                    gather_pass(table, GATHERED)

                @block.sync
                def _(sp):
                    def keep(i, slot):
                        sp.wait_ge(bank_copied, (i + 1) * UT)
                        sp.dma_start(kept[bass.ds(i, 1), :, :].rearrange("a p n -> p (a n)"), counts[:, slot, :]
                                     ).then_inc(stored[slot], 16)

                    def reload(r, slot):
                        sp.dma_start(counts[:, slot, :], kept[bass.ds(r, 1), :, :].rearrange("a p n -> p (a n)")
                                     ).then_inc(reloaded[slot], 16)

                    if making:
                        with sp.Fori(0, NU // 2) as it:
                            for h in range(2):
                                keep(it * 2 + h, h)
                        for u in range(2):
                            sp.wait_ge(stored[u], 16 * (NU // 2))
                    else:
                        for r in range(KSLOTS):
                            reload(r, r)
                        with sp.Fori(1, NU // KSLOTS) as it:
                            for u in range(KSLOTS):
                                sp.wait_ge(applied, (it - 1) * KSLOTS + (u + 1))
                                reload(it * KSLOTS + u, u)

                @block.vector
                def _(dve):
                    def pair_hot(i, b):
                        if not isinstance(i, int) or i >= 2:
                            dve.wait_ge(bank_full, UT * (i - 1))
                        one_hots(hot_src[:, b, :, :], iota_h, src_lo2, i * UT + T0)
                        one_hots(hot_pair[:, b, :, :], iota_h, pair2, i * UT + T0).then_inc(pair_ready, 1)

                    def reduce(k, b):
                        if not isinstance(k, int) or k >= 2:
                            dve.wait_ge(placed, k - 1)
                        nc.vector.tensor_scalar(place[:, b, :], diag_f[0:DW, :], offset[:, bass.ds(k, 1)],
                                                None, ALU.is_equal)
                        dve.wait_ge(applied, k + 1)
                        nc.vector.tensor_reduce(dsum[:, b, :], tp[0:DW, b, 0:3 * D].rearrange("p (a d) -> p d a", a=3),
                                                AX.X, ALU.add).then_inc(reduced, 1)

                    for j in range(R):
                        stage(j, j)
                    if making:
                        pair_hot(0, 0)
                        pair_hot(1, 1)
                    for k in range(EARLY):
                        if making:
                            pair_hot(k + 2, k % 2)
                        reduce(k, k % 2)
                        if k == 0:
                            window_hots(0, 0)

                    def turn(it, first, last):
                        for j in range(R):
                            g = it * R + j
                            if not (first and j == 0):
                                dve.wait_ge(summed, g)
                                if not last or j == 0:
                                    stage(g + (R - 1), (j - 1) % R)
                            if not (last and j == R - 1):
                                window_hots(g + 1, j + 1)
                            for h in range(j * BEHIND, (j + 1) * BEHIND):
                                k = it * IN_TURN + (EARLY + h)
                                if making and not (last and h >= IN_TURN - 2):
                                    pair_hot(k + 2, h % 2)
                                reduce(k, h % 2)

                    turn(0, True, False)
                    with dve.Fori(1, CTURNS - 1) as it:
                        turn(it, False, False)
                    turn(CTURNS - 1, False, True)

                @block.scalar
                def _(act):
                    def copy_counts(i, slot):
                        to = counts[:, slot, :].rearrange("p (k s n) -> p k s n", k=NB, s=UT)
                        for b in range(UT):
                            act.wait_ge(bank_full, i * UT + (b + 1))
                            nc.scalar.copy(to[:, :, b, :], mm[:, b % 2, 0:NB * SW].rearrange("p (k n) -> p k n", k=NB)
                                           ).then_inc(bank_copied, 1)

                    if making:
                        for u in range(2):
                            copy_counts(u, u)
                        with act.Fori(1, NU // 2) as it:
                            for u in range(2):
                                act.wait_ge(stored[u], it * 16)
                                copy_counts(it * 2 + u, u)

                @block.tensor
                def _(pe):
                    def count(i, b, t):
                        if t == 0:
                            pe.wait_ge(pair_ready, i + 1)
                        if t >= 2 or not isinstance(i, int) or i > 0:
                            pe.wait_ge(bank_copied, i * UT + (t - 1))
                        nc.tensor.matmul(mm[:, t % 2, 0:NB * SW], lhsT=hot_src[:, b, t, :], rhs=hot_pair[:, b, t, :],
                                         start=True, stop=True).then_inc(bank_full, 1)

                    def apply(slot, b, k0, k1):
                        for k in range(k0, k1):
                            last = nc.tensor.matmul(tp[0:DW, b, 0:3 * D], lhsT=counts[:, slot, k * DW:(k + 1) * DW],
                                                    rhs=parts[:, k, :, :].rearrange("p a d -> p (a d)"),
                                                    start=(k == 0), stop=(k == NB - 1))
                        if k1 == NB:
                            last.then_inc(applied, 1)

                    def put(k, b, at):
                        pe.wait_ge(reduced, k + 1)
                        for w in range(2):
                            last = nc.tensor.matmul(agg[:, bass.ds(at + w * D, D)], lhsT=place[:, b, w * P:(w + 1) * P],
                                                    rhs=dsum[:, b, :], start=False, stop=True, skip_group_check=True)
                        last.then_inc(placed, 1)

                    def apply_made(k, b, ahead):
                        for t in range(UT):
                            if ahead:
                                count(k + 1, 1 - b, t)
                            if t == 0:
                                pe.wait_ge(bank_copied, (k + 1) * UT)
                            apply(b, b, t * NB // UT, (t + 1) * NB // UT)

                    if making:
                        for t in range(UT):
                            count(0, 0, t)

                    def application(k, h, reloads, last=False):
                        if making:
                            apply_made(k, h % 2, not last)
                        else:
                            pe.wait_ge(reloaded[h % KSLOTS], reloads)
                            apply(h % KSLOTS, h % 2, 0, NB)

                    at = columns(unit_col, 0, EARLY)
                    for k in range(EARLY):
                        application(k, k, 16 * (k // KSLOTS + 1))
                        if k:
                            put(k - 1, 1 - k % 2, at[k - 1])

                    def turn(it, last):
                        at = columns(col, it * R, R)
                        to = columns(unit_col, it * IN_TURN + (EARLY - 1), IN_TURN)
                        for j in range(R):
                            scatter_rows(pe, it * R + j, j, at[j])
                            for h in range(j * BEHIND, (j + 1) * BEHIND):
                                k = it * IN_TURN + (EARLY + h)
                                application(k, h, it * (16 * IN_TURN // KSLOTS) + 16 * ((EARLY + h) // KSLOTS + 1),
                                            last and h == IN_TURN - 1)
                                put(k - 1, 1 - h % 2, to[h])

                    with pe.Fori(0, CTURNS - 1) as it:
                        turn(it, False)
                    turn(CTURNS - 1, True)
                    put(NU - 1, (NU - 1) % 2, columns(unit_col, NU - 1, 1)[0])

        def zero_sums():
            for b in range(0, AGGB * D, 512):
                n = min(512, AGGB * D - b)
                last = nc.tensor.matmul(agg[:, b:b + n], lhsT=zeros_b[:, 0:P], rhs=zeros_b[:, 0:n],
                                        start=True, stop=True, skip_group_check=True)
            return last

        def warm_up():
            for _ in range(WARM_UP):
                nc.tensor.matmul(mm[:, 1, 0:512], lhsT=zeros_b[:, 0:P], rhs=zeros_b[:, 0:512], start=True, stop=True)

        def clear_edge_sems(sp):
            for s in edge_sems:
                sp.sem_clear(s)

        def clear_gather_sems(pool):
            pool.dma_reset(range(gathered[0].num, gathered[-1].num + 1))
            for s in gathered:
                pool.sem_clear(s)

        def shift_windows():
            with nc.Block() as block:
                @block.sync
                def _(sp):
                    clear_edge_sems(sp)

                @block.gpsimd
                def _(pool):
                    clear_gather_sems(pool)

                @block.vector
                def _(dve):
                    nc.vector.tensor_scalar(rel[:], rel[:], float(-WIN), None, ALU.add)
                    nc.vector.tensor_scalar(col[:], col[:], 2 * D, (NB - 1) * D, ALU.add, ALU.min)

            with nc.Block() as block:
                @block.vector
                def _(dve):
                    twice(rel2, rel[:])

        def first_windows():
            with nc.Block() as block:
                @block.vector
                def _(dve):
                    nc.vector.tensor_copy(rel[:], rel0[:])
                    twice(rel2, rel0[:])
                    nc.vector.tensor_copy(col[:], col0[:])

        def convolve(table, which):
            outlying = nc.values_load(flag[0:1, 0:1], min_val=0, max_val=1)
            with nc.If(outlying < 1):
                convolution_pass(table, which)
            with nc.Else():
                edge_pass(table)
                with nc.Fori(0, SHIFTS):
                    shift_windows()
                    edge_pass(table)
                first_windows()

        def sum_over_edges(table, layer):
            message_pass(table, layer)
            outlying = nc.values_load(flag[0:1, 0:1], min_val=0, max_val=1)
            with nc.If(outlying > 0):
                with nc.Fori(0, SHIFTS):
                    shift_windows()
                    message_pass(table, layer)
                first_windows()

        def bcast(ap, n):
            return ap.unsqueeze(2).to_broadcast([P, ap.shape[1], n])

        def over(bias, n):
            return bias.unsqueeze(1).to_broadcast([P, n, D])

        def node_sems(name, kinds):
            return {k: sem(f"{name}_{k}") for k in kinds.split()}

        def split_dve(dve, q, c):
            if 1 <= c <= NC:
                k0, n = chunk(c - 1)
                dve.wait_ge(q["term1"], c)
                nc.vector.tensor_tensor(work[:, k0:k0 + n, :], tab[:, k0:k0 + n, :], parts[:, k0:k0 + n, 0, :],
                                        ALU.subtract).then_inc(q["rest"], 1)
            if c >= 2:
                k0, n = chunk(c - 2)
                dve.wait_ge(q["term2"], c - 1)
                nc.vector.tensor_tensor(parts[:, k0:k0 + n, 2, :], work[:, k0:k0 + n, :], parts[:, k0:k0 + n, 1, :],
                                        ALU.subtract).then_inc(q["final"], 1)

        def split_act(act, q, c):
            if c < NC:
                k0, n = chunk(c)
                act.wait_ge(q["rows"], c + 1)
                nc.scalar.copy(parts[:, k0:k0 + n, 0, :], tab[:, k0:k0 + n, :]).then_inc(q["term1"], 1)
            if 1 <= c <= NC:
                k0, n = chunk(c - 1)
                act.wait_ge(q["rest"], c)
                nc.scalar.copy(parts[:, k0:k0 + n, 1, :], work[:, k0:k0 + n, :]).then_inc(q["term2"], 1)

        s_fill = sem("s_fill")
        s_io = sem("s_io")
        s_const = sem("s_const")
        s_dst, s_src = sem("s_dst"), sem("s_src")
        s_dst_t, s_src_t = sem("s_dst_t"), sem("s_src_t")
        s_x, s_w = sem("s_x"), sem("s_w")
        s_dve = sem("s_dve")
        s_split = sem("s_split")
        s_flipped = sem("s_flipped")
        s_parts = sem("s_parts")
        s_hot = sem("s_hot")
        s_counted = sem("s_counted")
        s_lower, s_degrees = sem("s_lower"), sem("s_degrees")
        s_mean = sem("s_mean")
        s_centered = sem("s_centered")
        s_squares = sem("s_squares")
        s_ready = sem("s_ready")
        s_rooted = sem("s_rooted")
        s_lowest, s_lowest_t = sem("s_lowest"), sem("s_lowest_t")
        s_block, s_block_all = sem("s_block"), sem("s_block_all")
        s_rel = sem("s_rel")
        s_number = sem("s_number")
        s_offset = sem("s_offset")
        s_pair, s_turned = sem("s_pair"), sem("s_turned")
        s_far, s_far_all = sem("s_far"), sem("s_far_all")

        def bias_rows(b):
            return b.rearrange("(a n) -> a n", a=1).to_broadcast([P, D])

        def store_table(sp, q, table):
            view = table.rearrange("(p k) d -> p k d", k=NB)
            rows_ = parts[:, :, :, :].rearrange("p k a d -> p k (a d)") if table.shape[1] > D else tab
            for c in range(NC):
                k0, n = chunk(c)
                sp.wait_ge(q["final"], c + 1)
                sp.dma_start(view[:, k0:k0 + n, :], rows_[:, k0:k0 + n, :]).then_inc(q["out"], 16)
            sp.wait_ge(q["out"], 16 * NC)

        def transposed(b):
            return tp[:, b, 0:TPP * TP].rearrange("p (c m) -> p m c", c=TPP)

        def by_tile(to, half):
            return to[:, :, :, half].rearrange("p g t -> p (g t)").rearrange("p (m c) -> p m c", c=TPP)

        q0 = node_sems("first", "rows term1 rest term2 final out")
        with nc.Block() as block:
            @block.sync
            def _(sp):
                def in_order(to, of, s_idx):
                    full = (TP - 1) * TE
                    sp.dma_start(to[0:TP - 1, :], of[0:full].rearrange("(p n) -> p n", n=TE)).then_inc(s_idx, 16)
                    sp.dma_start(to[TP - 1:TP, 0:E - full], of[full:E].rearrange("(p n) -> p n", p=1)
                                 ).then_inc(s_idx, 16)

                sp.wait_ge(s_fill, 1)
                in_order(dst_t, dst, s_dst_t)
                sp.wait_ge(s_fill, 3)
                for to, of, s_idx in ((dst_i, dst, s_dst), (src_i, src, s_src)):
                    full = (NG - 1) * GE
                    sp.dma_start(to[:, 0:NG - 1, :], of[0:full].rearrange("(g p t) -> p g t", p=P, t=TPG)
                                 ).then_inc(s_idx, 16)
                    sp.dma_start(to[0:TFULL, NG - 1:NG, :], of[full:full + TFULL * TPG].rearrange(
                        "(p g t) -> p g t", g=1, t=TPG)).then_inc(s_idx, 16)
                    sp.dma_start(to[TFULL:TFULL + 1, NG - 1:NG, 0:TREST], of[E - TREST:E].rearrange(
                        "(p g t) -> p g t", p=1, g=1)).then_inc(s_idx, 16)
                in_order(src_t, src, s_src_t)
                sp.dma_start(W1_s[:], W1).then_inc(s_w, 16)
                sp.dma_start(W2_s[:], W2).then_inc(s_w, 16)
                sp.dma_start(b1_s[:], b1.rearrange("(p a) -> p a", a=1)).then_inc(s_w, 16)
                sp.dma_start(b2_s[:], bias_rows(b2)).then_inc(s_w, 16)
                for l, (wm, bm, wa, ba) in enumerate(((W1_msg, b1_msg, W1_app, b1_app),
                                                      (W2_msg, b2_msg, W2_app, b2_app))):
                    sp.dma_start(top_s[:, l, :], wm[0:D, :]).then_inc(s_w, 16)
                    sp.dma_start(bot_s[0:D, l, 0:D], wm[D:2 * D, :]).then_inc(s_w, 16)
                    sp.dma_start(bot_s[D:P, l, D:P], wm[D:2 * D, :]).then_inc(s_w, 16)
                    sp.dma_start(app_s[:, l, :], wa).then_inc(s_w, 16)
                    sp.dma_start(bmsg_s[:, l, :], bias_rows(bm)).then_inc(s_w, 16)
                    sp.dma_start(bapp_s[:, l, :], bias_rows(ba)).then_inc(s_w, 16)
                store_table(sp, q0, tables[0])
                sp.wait_ge(s_w, 16 * 16)

            @block.scalar
            def _(act):
                act.wait_ge(s_fill, 2)
                act.dma_start(xs[:, 0:NB - 1, :], x[0:(NB - 1) * P, :].rearrange("(k p) d -> p k d", p=P)
                              ).then_inc(s_x, 16)
                act.dma_start(xs[0:NTAIL, NB - 1, :], x[(NB - 1) * P:N, :]).then_inc(s_x, 16)
                for b, to in enumerate((dst_lo2, dst_hi2)):
                    act.wait_ge(s_flipped, b + 1)
                    for half in range(2):
                        last = nc.scalar.copy(by_tile(to, half), transposed(b))
                last.then_inc(s_parts, 1)
                act.wait_ge(s_mean, 1)
                for k in range(NB):
                    last = nc.scalar.activation(work[:, k, :], xs[:, k, :], ACT.Identity, bias=stat[:, 0, k:k + 1])
                last.then_inc(s_centered, 1)
                act.wait_ge(s_centered, 1)
                nc.scalar.activation(tab[:], work[:], ACT.Square).then_inc(s_squares, 1)
                act.wait_ge(s_ready, 1)
                nc.scalar.activation(stat[:, 2, :], stat[:, 2, :], ACT.Sqrt).then_inc(s_rooted, 1)
                act.wait_ge(s_ready, 2)
                nc.scalar.activation(dis[:], dis[:], ACT.Sqrt).then_inc(s_rooted, 1)
                act.wait_ge(s_ready, 3)
                for c in range(NC + 1):
                    if c < NC:
                        k0, n = chunk(c)
                        for k in range(k0, k0 + n):
                            last = nc.scalar.activation(tab[:, k, :], work[:, k, :], ACT.Relu, scale=scale[:, k:k + 1])
                        last.then_inc(q0["rows"], 1)
                    split_act(act, q0, c)
                    if c == 2:
                        act.wait_ge(s_rel, 1)
                        for to in (rel[:], rel2[:, :, :, 0], rel2[:, :, :, 1]):
                            nc.scalar.copy(to, rel0[:])
                act.wait_ge(s_turned, 1)
                for b, to in enumerate((pair2, src_lo2)):
                    for half in range(2):
                        nc.scalar.copy(by_tile(to, half), transposed(b))

            @block.gpsimd
            def _(pool):
                nc.gpsimd.iota(iota_i[:], [[1, NB * SW]], base=0, channel_multiplier=0).then_inc(s_io, 1)
                nc.gpsimd.iota(part_i[:], [[1, 1]], base=0, channel_multiplier=1).then_inc(s_io, 1)
                nc.gpsimd.iota(diag_i[:], [[1, WIN]], base=0, channel_multiplier=-1).then_inc(s_io, 1)
                nc.gpsimd.iota(behind_i[:], [[1, TPP], [-UT, NU]], base=-T0, channel_multiplier=TPP).then_inc(s_io, 1)
                nc.gpsimd.iota(tile_i[:].rearrange("p (s n) -> p s n", s=UT), [[1, UT], [0, SW]], base=0,
                               channel_multiplier=0).then_inc(s_io, 1)
                pool.wait_ge(s_w, 16 * 16)
                pool.wait_ge(s_centered, 1)
                nc.gpsimd.tensor_tensor(xs[:], xs[:], over(b2_s[:], NB), ALU.add)

            @block.vector
            def _(dve):
                chain = Chain(dve, s_dve)
                past = E - (TP - 1) * TE
                nc.vector.memset(dst_t[96:TP, past:TE], NO_NODE).then_inc(s_fill, 1)
                nc.vector.memset(src_t[96:TP, past:TE], 0)
                nc.vector.memset(xs[:, NB - 1, :], 0.0).then_inc(s_fill, 1)
                nc.vector.memset(src_i[:, NG - 1, :], 0)
                nc.vector.memset(dst_i[:, NG - 1, :], NO_NODE)
                nc.vector.memset(bot_s[:], 0.0).then_inc(s_fill, 1)
                nc.vector.memset(row_i[:], 0)
                nc.vector.memset(zeros_b[:], 0.0)
                nc.vector.memset(ones[:], 1.0)
                dve.wait_ge(s_io, 5)
                nc.vector.tensor_copy(diag_f[:], diag_i[:])
                nc.vector.tensor_copy(iota_f[:], iota_i[:, 0:P])
                nc.vector.tensor_copy(iota_b[:], iota_i[:, 0:WIN])
                nc.vector.tensor_copy(iota_h[:], iota_i[:])
                for half in range(2):
                    nc.vector.tensor_copy(block2[:, :, half], iota_i[:, 1:NB + 1])
                chain(nc.vector.tensor_copy(part_f[:], part_i[:]))
                nc.vector.tensor_scalar(up[:], diag_f[0:HALF, 0:P], float(HALF), None, ALU.is_equal)
                nc.vector.tensor_scalar(ident[:], iota_f[:, 0:P], part_f[:], None, ALU.is_equal).then_inc(s_const, 1)
                chain(nc.vector.tensor_copy(behind[:], behind_i[:]))
                nc.vector.tensor_copy(tile_f[:], tile_i[:])
                nc.vector.tensor_scalar(opens[:], behind[:], 0.0, None, ALU.is_equal)
                chain(nc.vector.tensor_scalar(member[:], behind[:], 0.0, None, ALU.is_ge))
                chain(nc.vector.scalar_tensor_tensor(member[:], behind[:], float(UT), member[:], ALU.is_lt, ALU.mult))
                chain(nc.vector.tensor_tensor(behind[:], behind[:], member[:], ALU.mult))
                chain(nc.vector.tensor_reduce(number[:], behind[:], AX.X, ALU.add))
                for b in range(TPP):
                    nc.vector.tensor_scalar(of_tile[:, b, :], tile_f[:], number[:, b:b + 1], None, ALU.is_equal)
                dve.wait_ge(s_dst_t, 32)
                chain(nc.vector.tensor_scalar(tmp_t[:].bitcast(i32), dst_t[:], HALF - 1, None, ALU.bitwise_and))
                chain(nc.vector.tensor_copy(lo_t[:], tmp_t[:].bitcast(i32)))
                dve.sem_inc(s_split, 1)
                chain(nc.vector.tensor_scalar(tmp_t[:].bitcast(i32), dst_t[:], 6, None, ALU.arith_shift_right))
                nc.vector.tensor_copy(pair_t[:], tmp_t[:].bitcast(i32)).then_inc(s_split, 1)
                dve.wait_ge(s_x, 32)
                chain(nc.vector.tensor_reduce(stat[:, 0, :], xs[:], AX.X, ALU.add))
                nc.vector.tensor_scalar(stat[:, 0, :], stat[:, 0, :], -1.0 / D, None, ALU.mult).then_inc(s_mean, 1)
                dve.wait_ge(s_parts, 1)

                def degree_hot(i, b):
                    one_hots(hot_lo[:, b, :, :], iota_h, dst_lo2, i * (DG * TPG))
                    one_hots(hot_hi[:, b, :, :], iota_h, dst_hi2, i * (DG * TPG)).then_inc(s_hot, 1)

                def degree_hots(first, last):
                    with dve.Fori(0, (last - first) // 2) as it:
                        for h in range(2):
                            dve.wait_ge(s_counted, it * 2 + (first + h - 1))
                            degree_hot(it * 2 + (first + h), (first + h) % 2)

                degree_hot(0, 0)
                degree_hot(1, 1)
                dve.wait_ge(s_counted, 1)
                degree_hot(2, 0)
                degree_hots(3, 7)
                dve.wait_ge(s_squares, 1)
                chain(nc.vector.tensor_reduce(stat[:, 1, :], tab[:], AX.X, ALU.add))
                nc.vector.tensor_scalar(stat[:, 2, :], stat[:, 1, :], 1.0 / D, EPS, ALU.mult, ALU.add).then_inc(s_ready, 1)
                degree_hots(7, NG // DG)
                dve.wait_ge(s_counted, NG // DG)
                nc.vector.tensor_copy(lower[:], mm[0:HALF, 0, 0:2 * NB]).then_inc(s_lower, 1)
                dve.wait_ge(s_degrees, 1)
                nc.vector.tensor_scalar(dis[:], mm[:, 1, 0:NB], 1.0, None, ALU.add).then_inc(s_ready, 1)
                dve.wait_ge(s_rooted, 2)
                nc.vector.reciprocal(stat[:, 3, :], stat[:, 2, :])
                chain(nc.vector.reciprocal(dis[:], dis[:]))
                nc.vector.tensor_tensor(scale[:], stat[:, 3, :], dis[:], ALU.mult).then_inc(s_ready, 1)
                dve.wait_ge(s_dst, 48)
                nc.vector.tensor_copy(dst_f[:], dst_i[:])
                dve.wait_ge(s_src, 48)
                chain(nc.vector.tensor_scalar(tmp_i[:], src_i[:], P - 1, None, ALU.bitwise_and))
                nc.vector.tensor_copy(ident_b[:], ident[:])
                chain(nc.vector.tensor_copy(pe_lo[:], tmp_i[:, :, TPG - PE_TILES:TPG]))
                chain(nc.vector.tensor_scalar(tmp_i[:], tmp_i[:], NB, None, ALU.mult))
                chain(nc.vector.tensor_scalar(src_i[:], src_i[:], 7, None, ALU.arith_shift_right))
                nc.vector.tensor_tensor(row_i[:, 0:NG, :], src_i[:], tmp_i[:], ALU.add)
                nc.vector.tensor_scalar(pe_hi[:], src_i[:, :, TPG - PE_TILES:TPG], 1, None, ALU.add)
                chain(nc.vector.tensor_reduce(gmin[:], dst_f[:], AX.X, ALU.min))
                dve.sem_inc(s_lowest, 1)
                split_dve(dve, q0, 1)
                dve.wait_ge(s_lowest_t, 1)
                chain(nc.vector.tensor_reduce(bmin[:, 1:2], tp[0:NG, 0, 0:P], AX.X, ALU.min))
                chain(nc.vector.tensor_copy(bmin_i[:], bmin[:, 1:2]))
                chain(nc.vector.tensor_scalar(bmin_i[:], bmin_i[:], 7, None, ALU.arith_shift_right))
                chain(nc.vector.tensor_copy(bmin[:, 0:1], bmin_i[:]))
                nc.vector.tensor_scalar(bdiag[:], ident[0:NG, 0:NG], bmin[:, 0:1], None, ALU.mult).then_inc(s_block, 1)
                dve.wait_ge(s_block_all, 1)
                nc.vector.tensor_scalar(base[:], mm[:, 1, 0:NG], float(P), None, ALU.mult)
                for to in (col0, col):
                    last = nc.vector.tensor_scalar(to[:], mm[0:1, 1, 0:NG], float(D), float((NB - 1) * D),
                                                   ALU.mult, ALU.min)
                chain(last)
                chain(nc.vector.tensor_tensor(rel0[:], dst_f[:], bcast(base[:], TPG), ALU.subtract))
                dve.sem_inc(s_rel, 1)
                split_dve(dve, q0, 2)
                chain(nc.vector.tensor_scalar(outside[:], dst_f[:], float(NO_NODE), None, ALU.is_lt))
                chain(nc.vector.scalar_tensor_tensor(outside[:], rel0[:], float(WIN), outside[:], ALU.is_ge, ALU.mult))
                nc.vector.tensor_reduce(far[:], outside[:], AX.XY, ALU.max)
                split_dve(dve, q0, 3)
                tiles_dst, tiles_behind = (m[:].rearrange("p (b n) -> p b n", b=TPP) for m in (tmp_t, pair_t))
                chain(nc.vector.tensor_copy(tmp_t[:], dst_t[:]))
                chain(nc.vector.tensor_reduce(first_t[:], tiles_dst, AX.X, ALU.min))
                nc.vector.tensor_scalar(lo_t[:], tmp_t[:], float(NO_NODE), None, ALU.is_lt)
                chain(nc.vector.tensor_tensor(tiles_behind, tiles_dst,
                                              first_t[:].unsqueeze(2).to_broadcast([TP, TPP, P]), ALU.subtract))
                chain(nc.vector.scalar_tensor_tensor(lo_t[:], pair_t[:], float(SW), lo_t[:], ALU.is_ge, ALU.mult))
                nc.vector.tensor_reduce(far_t[:], lo_t[:], AX.X, ALU.max)
                chain(nc.vector.tensor_copy(block_i[:], first_t[:]))
                chain(nc.vector.tensor_scalar(block_i[:], block_i[:], -P, None, ALU.bitwise_and))
                nc.vector.tensor_copy(block_t[:], block_i[:])
                chain(nc.vector.scalar_tensor_tensor(first_t[:], number[:], float(-SW), first_t[:], ALU.mult, ALU.add))
                for b in range(TPP):
                    nc.vector.tensor_scalar(of_unit[:, b, :], member[:, b, :], first_t[:, b:b + 1], None, ALU.mult)
                    last = nc.vector.tensor_scalar(opens[:, b, :], opens[:, b, :], block_t[:, b:b + 1], -1.0,
                                                   ALU.mult, ALU.mult)
                last.then_inc(s_number, 1)
                split_dve(dve, q0, 4)
                chain(nc.vector.tensor_scalar(tmp_t[:], pair_t[:], float(SW), FAR, ALU.is_ge, ALU.mult))
                chain(nc.vector.scalar_tensor_tensor(pair_t[:], pair_t[:], float(SW), tmp_t[:], ALU.min, ALU.add))
                dve.wait_ge(s_src_t, 32)
                chain(nc.vector.tensor_scalar(dst_t[:], src_t[:], P - 1, None, ALU.bitwise_and))
                nc.vector.tensor_copy(lo_t[:], dst_t[:])
                chain(nc.vector.tensor_scalar(src_t[:], src_t[:], 7, None, ALU.arith_shift_right))
                chain(nc.vector.tensor_copy(tmp_t[:], src_t[:]))
                nc.vector.scalar_tensor_tensor(pair_t[:], tmp_t[:], float(SW), pair_t[:], ALU.mult, ALU.add
                                               ).then_inc(s_pair, 1)
                split_dve(dve, q0, 5)
                dve.wait_ge(s_offset, 1)
                nc.vector.tensor_copy(offset[:], mm[0:DW, 1, 0:NU])
                nc.vector.tensor_scalar(unit_col[:], mm[0:1, 1, 64:64 + NU], -float(D) / P, float((NB - 1) * D),
                                        ALU.mult, ALU.min)
                chain(nc.vector.tensor_scalar(target[:], mm[0:DW, 1, 0:NU], part_f[0:DW, :], None, ALU.add))
                chain(nc.vector.tensor_scalar(target_far[:], target[:], float(WIN), None, ALU.is_ge))
                chain(nc.vector.scalar_tensor_tensor(target_far[:], target[:], 0.0, target_far[:], ALU.is_lt, ALU.max))
                nc.vector.tensor_reduce(far_u[:], target_far[:], AX.X, ALU.max).then_inc(s_far, 1)
                dve.wait_ge(s_far_all, 1)
                chain(nc.vector.tensor_copy(farT[:], mm[0:1, 1, 128:129]))
                nc.vector.tensor_scalar(flag[:], farT[:], 0.0, None, ALU.is_gt)
                for c in range(6, NC + 2):
                    split_dve(dve, q0, c)

            @block.tensor
            def _(pe):
                pe.wait_ge(s_const, 1)
                for b, m in enumerate((lo_t, pair_t)):
                    pe.wait_ge(s_split, b + 1)
                    for c in range(TPP):
                        last = nc.tensor.transpose(tp[:, b, c * TP:(c + 1) * TP], m[:, c * P:(c + 1) * P],
                                                   ident[0:TP, 0:TP])
                    last.then_inc(s_flipped, 1)
                nc.tensor.matmul(mm[0:HALF, 0, 0:2 * NB], lhsT=zeros_b[:, 0:HALF], rhs=zeros_b[:, 0:2 * NB],
                                 start=True, stop=True)

                def degrees(i, b):
                    pe.wait_ge(s_hot, i + 1)
                    for t in range(DG * TPG):
                        last = nc.tensor.matmul(mm[0:HALF, 0, 0:2 * NB], lhsT=hot_lo[:, b, t, :],
                                                rhs=hot_hi[:, b, t, :], start=False, stop=True, skip_group_check=True)
                    last.then_inc(s_counted, 1)

                degrees(0, 0)
                with pe.Fori(0, NG // DG // 2) as it:
                    for h in range(2):
                        degrees(it * 2 + (h + 1), 1 - h)
                pe.wait_ge(s_lower, 1)
                nc.tensor.matmul(mm[:, 1, 0:NB], lhsT=ident[0:HALF, :], rhs=lower[:, 0:2 * NB:2], start=True, stop=False)
                nc.tensor.matmul(mm[:, 1, 0:NB], lhsT=up[:], rhs=lower[:, 1:2 * NB:2], start=False, stop=True
                                 ).then_inc(s_degrees, 1)
                pe.wait_ge(s_lowest, 1)
                nc.tensor.transpose(tp[0:NG, 0, 0:P], gmin[:], ident[:]).then_inc(s_lowest_t, 1)
                pe.wait_ge(s_block, 1)
                nc.tensor.matmul(mm[:, 1, 0:NG], lhsT=ones[0:NG, :], rhs=bdiag[:], start=True, stop=True).then_inc(s_block_all, 1)
                pe.wait_ge(s_number, 1)
                for b in range(TPP):
                    nc.tensor.matmul(mm[0:DW, 1, 0:NU], lhsT=of_tile[:, b, :], rhs=of_unit[:, b, :],
                                     start=(b == 0), stop=False)
                    nc.tensor.matmul(mm[0:DW, 1, 0:NU], lhsT=ones[0:TP, 0:DW], rhs=opens[:, b, :],
                                     start=False, stop=(b == TPP - 1))
                for b in range(TPP):
                    last = nc.tensor.matmul(mm[0:1, 1, 64:64 + NU], lhsT=ones[0:TP, 0:1], rhs=opens[:, b, :],
                                            start=(b == 0), stop=(b == TPP - 1))
                last.then_inc(s_offset, 1)
                pe.wait_ge(s_pair, 1)
                for b, m in enumerate((pair_t, lo_t)):
                    for c in range(TPP):
                        last = nc.tensor.transpose(tp[:, b, c * TP:(c + 1) * TP], m[:, c * P:(c + 1) * P],
                                                   ident[0:TP, 0:TP])
                last.then_inc(s_turned, 1)
                pe.wait_ge(s_far, 1)
                for b, (m, n) in enumerate(((far, P), (far_t, TP), (far_u, DW))):
                    last = nc.tensor.matmul(mm[0:1, 1, 128:129], lhsT=m[:], rhs=ones[0:n, 0:1],
                                            start=(b == 0), stop=(b == 2))
                last.then_inc(s_far_all, 1)
                zero_sums()

        def turn_chunk(q, c, source, wide):
            k0, n = chunk(c)
            for i in range(n):
                last = nc.tensor.transpose(tp[0:(2 * D if wide else D), c % 2, i * P:(i + 1) * P],
                                           source[:, k0 + i, :], ident[:])
            last.then_inc(q["turned"], 1)

        def copy_chunk(q, c, wide):
            k0, n = chunk(c)
            h = 2 * D if wide else D
            nc.scalar.copy(catT[0:h, k0 * P:(k0 + n) * P], tp[0:h, c % 2, 0:n * P]).then_inc(q["copied"], 1)

        def product_chunk(q, c, weights, rows_):
            k0, n = chunk(c)
            for i in range(n):
                last = nc.tensor.matmul(mm[:, c % 2, i * D:(i + 1) * D], lhsT=catT[0:rows_, (k0 + i) * P:(k0 + i + 1) * P],
                                        rhs=weights, start=True, stop=True)
            last.then_inc(q["done"], 1)

        def product(c):
            n = chunk(c)[1]
            return mm[:, c % 2, 0:n * D].rearrange("p (k d) -> p k d", d=D)

        def pe_sweep(pe, q, source, weights, wide, before=None):
            for c in range(NC + 1):
                if c < NC:
                    pe.wait_ge(q["ready"], c + 1)
                    if c >= 2:
                        pe.wait_ge(q["copied"], c - 1)
                    elif before is not None:
                        pe.wait_ge(before["copied"], NC)
                    turn_chunk(q, c, source, wide)
                if c >= 1:
                    pe.wait_ge(q["copied"], c)
                    if c >= 3:
                        pe.wait_ge(q["final"], c - 2)
                    elif before is not None:
                        pe.wait_ge(before["final"], NC)
                    product_chunk(q, c - 1, weights, 2 * D if wide else D)

        def act_sweep(act, q, wide):
            for c in range(NC):
                act.wait_ge(q["turned"], c + 1)
                copy_chunk(q, c, wide)

        convolve(tables[0], 0)
        q = node_sems("gcn1", "dve ready turned copied mid relu done rows term1 rest term2 final out")
        with nc.Block() as block:
            @block.sync
            def _(sp):
                clear_edge_sems(sp)
                store_table(sp, q, tables[1])

            @block.gpsimd
            def _(pool):
                clear_gather_sems(pool)

            @block.vector
            def _(dve):
                chain = Chain(dve, q["dve"])
                for c in range(NC):
                    k0, n = chunk(c)
                    w = work[:, k0:k0 + n, :]
                    chain(nc.vector.tensor_tensor(w, agg_chunk(c), tab[:, k0:k0 + n, :], ALU.add))
                    nc.vector.tensor_tensor(w, w, bcast(dis[:, k0:k0 + n], D), ALU.mult).then_inc(q["ready"], 1)
                for c in range(NC + 2):
                    if c < NC:
                        k0, n = chunk(c)
                        dve.wait_ge(q["done"], c + 1)
                        nc.vector.tensor_tensor(tab[:, k0:k0 + n, :], agg[:, c % 4 * 512:c % 4 * 512 + n * D].rearrange(
                            "p (k d) -> p k d", d=D), bcast(dis[:, k0:k0 + n], D), ALU.mult).then_inc(q["rows"], 1)
                    split_dve(dve, q, c)

            @block.scalar
            def _(act):
                for c in range(NC + 3):
                    if c < NC:
                        act.wait_ge(q["turned"], c + 1)
                        copy_chunk(q, c, False)
                    if 1 <= c <= NC:
                        k0, n = chunk(c - 1)
                        act.wait_ge(q["mid"], c)
                        nc.scalar.activation(midT[:, k0 * P:(k0 + n) * P], mm[:, (c - 1) % 2, 0:n * P], ACT.Relu,
                                             bias=b1_s[:]).then_inc(q["relu"], 1)
                    if c >= 2:
                        split_act(act, q, c - 2)

            @block.tensor
            def _(pe):
                warm_up()
                for c in range(NC + 2):
                    if c < NC:
                        pe.wait_ge(q["ready"], c + 1)
                        if c >= 2:
                            pe.wait_ge(q["copied"], c - 1)
                        turn_chunk(q, c, work, False)
                    if 1 <= c <= NC:
                        k0, n = chunk(c - 1)
                        pe.wait_ge(q["copied"], c)
                        if c >= 3:
                            pe.wait_ge(q["relu"], c - 2)
                        nc.tensor.matmul(mm[:, (c - 1) % 2, 0:n * P], lhsT=W1_s[:], rhs=catT[0:D, k0 * P:(k0 + n) * P],
                                         start=True, stop=True).then_inc(q["mid"], 1)
                    if c >= 2:
                        k0, n = chunk(c - 2)
                        pe.wait_ge(q["relu"], c - 1)
                        pe.wait_ge(q["ready"], min(NC, 2 * (c - 1)))
                        if c >= 6:
                            pe.wait_ge(q["rows"], c - 5)
                        for i in range(n):
                            k = k0 + i
                            at = (c - 2) % 4 * 512 + i * D
                            last = nc.tensor.matmul(agg[:, at:at + D], lhsT=midT[:, k * P:(k + 1) * P],
                                                    rhs=W2_s[:], start=True, stop=True, skip_group_check=True)
                        last.then_inc(q["done"], 1)
                pe.wait_ge(q["final"], NC)
                zero_sums()

        convolve(tables[1], 1)
        q2 = node_sems("gcn2", "dve ready turned copied done final out")
        q2s = dict(node_sems("split2", "term1 rest term2 final"), rows=q2["final"])
        centered, squared, varied, rooted, scaled = (sem(f"ln_{k}") for k in (
            "centered", "squared", "varied", "rooted", "scaled"))
        with nc.Block() as block:
            @block.sync
            def _(sp):
                clear_edge_sems(sp)
                store_table(sp, q2, tables[2])

            @block.gpsimd
            def _(pool):
                clear_gather_sems(pool)

            @block.vector
            def _(dve):
                chain = Chain(dve, q2["dve"])
                nc.vector.memset(rows[:, :, (TPG - PE_TILES) * D:TPG * D], 0.0)
                for c in range(NC + 7):
                    if c < NC:
                        k0, n = chunk(c)
                        w, x_, mean = work[:, k0:k0 + n, :], xs[:, k0:k0 + n, :], stat[:, 0, k0:k0 + n]
                        chain(nc.vector.tensor_tensor(w, agg_chunk(c), tab[:, k0:k0 + n, :], ALU.add))
                        chain(nc.vector.tensor_tensor(w, w, bcast(dis[:, k0:k0 + n], D), ALU.mult))
                        chain(nc.vector.tensor_tensor(x_, x_, w, ALU.add))
                        chain(nc.vector.tensor_reduce(mean, x_, AX.X, ALU.add))
                        chain(nc.vector.tensor_scalar(mean, mean, 1.0 / D, None, ALU.mult))
                        nc.vector.tensor_tensor(w, x_, bcast(mean, D), ALU.subtract).then_inc(centered, 1)
                    if 1 <= c <= NC:
                        k0, n = chunk(c - 1)
                        dve.wait_ge(squared, c)
                        chain(nc.vector.tensor_reduce(stat[:, 1, k0:k0 + n], tab[:, k0:k0 + n, :], AX.X, ALU.add))
                        nc.vector.tensor_scalar(stat[:, 1, k0:k0 + n], stat[:, 1, k0:k0 + n], 1.0 / D, EPS,
                                                ALU.mult, ALU.add).then_inc(varied, 1)
                    if 2 <= c <= NC + 1:
                        k0, n = chunk(c - 2)
                        dve.wait_ge(rooted, c - 1)
                        nc.vector.reciprocal(scale[:, k0:k0 + n], stat[:, 2, k0:k0 + n]).then_inc(scaled, 1)
                    if 5 <= c < NC + 5:
                        k0, n = chunk(c - 5)
                        dve.wait_ge(q2["done"], c - 4)
                        nc.vector.tensor_tensor(tab[:, k0:k0 + n, :], product(c - 5), over(bmsg_s[:, 0, :], n),
                                                ALU.add).then_inc(q2["final"], 1)
                    if c >= 5:
                        split_dve(dve, q2s, c - 5)

            @block.scalar
            def _(act):
                for c in range(NC + 7):
                    if c < NC:
                        k0, n = chunk(c)
                        act.wait_ge(centered, c + 1)
                        nc.scalar.activation(tab[:, k0:k0 + n, :], work[:, k0:k0 + n, :], ACT.Square
                                             ).then_inc(squared, 1)
                    if 1 <= c <= NC:
                        k0, n = chunk(c - 1)
                        act.wait_ge(varied, c)
                        nc.scalar.activation(stat[:, 2, k0:k0 + n], stat[:, 1, k0:k0 + n], ACT.Sqrt
                                             ).then_inc(rooted, 1)
                    if 2 <= c <= NC + 1:
                        k0, n = chunk(c - 2)
                        act.wait_ge(scaled, c - 1)
                        for k in range(k0, k0 + n):
                            last = nc.scalar.activation(cat[:, k, 0:D], work[:, k, :], ACT.Relu, scale=scale[:, k:k + 1])
                        last.then_inc(q2["ready"], 1)
                    if 3 <= c < NC + 3:
                        act.wait_ge(q2["turned"], c - 2)
                        copy_chunk(q2, c - 3, False)
                    if c >= 6:
                        split_act(act, q2s, c - 6)

            @block.tensor
            def _(pe):
                pe_sweep(pe, q2, cat[:, :, 0:D], top_s[:, 0, :], False)
                pe.wait_ge(centered, NC)
                zero_sums()

        def gather_sums(q):
            for c in range(NC):
                k0, n = chunk(c)
                nc.vector.tensor_copy(cat[:, k0:k0 + n, D:2 * D], agg_chunk(c)).then_inc(q["ready"], 1)

        def apply_chunk(dve, chain, q, layer, c, to):
            k0, n = chunk(c)
            dve.wait_ge(q["done"], c + 1)
            w = work[:, k0:k0 + n, :]
            chain(nc.vector.tensor_tensor(w, product(c), over(bapp_s[:, layer, :], n), ALU.add))
            return nc.vector.scalar_tensor_tensor(to, w, 0.0, cat[:, k0:k0 + n, 0:D], ALU.max, ALU.add)

        sum_over_edges(tables[2], 0)
        q3 = node_sems("app1", "dve ready turned copied done final")
        q4 = node_sems("msg2", "turned copied done final out")
        q4s = dict(node_sems("split4", "term1 rest term2 final"), rows=q4["final"])
        with nc.Block() as block:
            @block.sync
            def _(sp):
                clear_edge_sems(sp)
                store_table(sp, q4, tables[3])

            @block.gpsimd
            def _(pool):
                clear_gather_sems(pool)

            @block.vector
            def _(dve):
                chain = Chain(dve, q3["dve"])
                gather_sums(q3)
                for c in range(NC):
                    k0, n = chunk(c)
                    apply_chunk(dve, chain, q3, 0, c, cat[:, k0:k0 + n, 0:D]).then_inc(q3["final"], 1)
                for c in range(NC):
                    k0, n = chunk(c)
                    dve.wait_ge(q4["done"], c + 1)
                    nc.vector.tensor_tensor(tab[:, k0:k0 + n, :], product(c), over(bmsg_s[:, 1, :], n),
                                            ALU.add).then_inc(q4["final"], 1)
                for c in range(1, NC + 2):
                    split_dve(dve, q4s, c)

            @block.scalar
            def _(act):
                act_sweep(act, q3, True)
                act_sweep(act, q4, False)
                for c in range(NC + 1):
                    split_act(act, q4s, c)

            @block.tensor
            def _(pe):
                warm_up()
                pe.wait_ge(q3["ready"], NC)
                zero_sums()
                pe_sweep(pe, q3, cat, app_s[:, 0, :], True)
                pe_sweep(pe, dict(q4, ready=q3["final"]), cat[:, :, 0:D], top_s[:, 1, :], False, before=q3)

        sum_over_edges(tables[3], 1)
        q5 = node_sems("app2", "dve ready turned copied done final out")
        with nc.Block() as block:
            @block.sync
            def _(sp):
                for c in range(NC):
                    k0, n = chunk(c)
                    sp.wait_ge(q5["final"], c + 1)
                    if c < NC - 1:
                        sp.dma_start(out[k0 * P:(k0 + n) * P, :].rearrange("(k p) d -> p k d", p=P),
                                     work[:, k0:k0 + n, :]).then_inc(q5["out"], 16)
                    else:
                        sp.dma_start(out[k0 * P:N, :], work[0:NTAIL, k0, :]).then_inc(q5["out"], 16)
                sp.wait_ge(q5["out"], 16 * NC)

            @block.vector
            def _(dve):
                chain = Chain(dve, q5["dve"])
                gather_sums(q5)
                for c in range(NC):
                    k0, n = chunk(c)
                    w = work[:, k0:k0 + n, :]
                    chain(apply_chunk(dve, chain, q5, 1, c, w))
                    nc.vector.tensor_tensor(w, w, xs[:, k0:k0 + n, :], ALU.add).then_inc(q5["final"], 1)

            @block.scalar
            def _(act):
                act_sweep(act, q5, True)

            @block.tensor
            def _(pe):
                warm_up()
                pe_sweep(pe, q5, cat, app_s[:, 1, :], True)


_INS = ['x', 'src', 'dst', 'edge_attr_64', 'L0_gnn_W1', 'L0_gnn_b1', 'L0_gnn_W2', 'L0_gnn_b2',
        'L1_gnn_W1_msg', 'L1_gnn_b1_msg', 'L1_gnn_W1_app', 'L1_gnn_b1_app',
        'L1_gnn_W2_msg', 'L1_gnn_b2_msg', 'L1_gnn_W2_app', 'L1_gnn_b2_app']
_OUT = (3125, 64)


def kernel(**inputs):
    import numpy as _np
    import concourse.bacc as _bacc
    from concourse import mybir as _mybir
    from concourse.bass_utils import run_bass_kernel_spmd as _run

    nc = _bacc.Bacc("TRN2", target_bir_lowering=False, num_devices=1)
    arrays, args = {}, []
    for name in _INS:
        a = _np.ascontiguousarray(inputs[name])
        arrays[f"in_{name}_dram"] = a
        args.append(nc.dram_tensor(f"in_{name}_dram", a.shape, _mybir.dt.from_np(a.dtype), kind="ExternalInput").ap())
    args.append(nc.dram_tensor("out_0_dram", _OUT, _mybir.dt.float32, kind="ExternalOutput").ap())
    gnn_kernel(nc, *args)
    r = _run(nc, [arrays], core_ids=[0])
    return r.results[0]["out_0_dram"]
```
